# Optimizing a Trainium2 kernel written in Bass

```python
import numpy as np
import jax
import jax.numpy as jnp

def _softmax(x, axis=-1):
    return jax.nn.softmax(x, axis=axis)

def _gelu(x):
    return jax.nn.gelu(x, approximate=True)

def _silu(x):
    return jax.nn.silu(x)

def _sigmoid(x):
    return jax.nn.sigmoid(x)

def _layernorm(x, axis=-1, eps=1e-05):
    m = jnp.mean(x, axis=axis, keepdims=True)
    v = jnp.var(x, axis=axis, keepdims=True)
    return (x - m) / jnp.sqrt(v + eps)

def _scatter_add(tgt, idx, src, axis=0):
    return tgt.at[idx].add(src)

def _segment_sum(src, seg, n):
    return jax.ops.segment_sum(src, seg, n)
kernel_name = 'mk_adj_resnorm_d2_adj_r2_b72ab8'

def setup_inputs(seed: int=0):
    np.random.seed(seed)
    _w = jnp.asarray

    def _rec_inputs():
        import jax
        import jax.numpy as jnp
        _gk = jax.random.key(seed)
        x = -0.0002928 + 1 * jax.random.normal(jax.random.fold_in(_gk, 1), (128, 128, 256), jnp.float32)
        _a = jax.random.bernoulli(jax.random.fold_in(_gk, 2), 0.0625, (128, 128, 128))
        _a = jnp.logical_or(_a, jnp.swapaxes(_a, -1, -2))
        _a = jnp.logical_or(_a, jnp.eye(128, dtype=bool))
        _af = _a.astype(jnp.float32)
        _af = _af * jax.random.uniform(jax.random.fold_in(_gk, 3), (128, 128, 128), jnp.float32, 0.05, 1)
        adj = _af
        return (x, adj)
    x, adj = _rec_inputs()

    def _L0_gnn_setup():
        import jax, jax.numpy as jnp
        import numpy as np
        B, N, DIN, DOUT, K = (4, 1024, 256, 256, 3)
        key = jax.random.key(seed)
        ks = jax.random.split(key, 8)
        X = jax.random.normal(ks[0], (B, N, DIN), dtype=jnp.float32)
        A = jax.random.uniform(ks[1], (B, N, N), dtype=jnp.float32)
        Wv = jax.random.normal(ks[2], (DIN, DOUT), dtype=jnp.float32) * 0.02
        bv = jax.random.normal(ks[3], (DOUT,), dtype=jnp.float32) * 0.02
        aw = jax.random.normal(ks[4], (2 * DOUT, 1), dtype=jnp.float32) * 0.05
        ab = jax.random.normal(ks[5], (1,), dtype=jnp.float32) * 0.05
        Wk = jax.random.normal(ks[6], (K, DIN, DOUT), dtype=jnp.float32) * 0.02
        bk = jax.random.normal(ks[7], (K, DOUT), dtype=jnp.float32) * 0.02
        return {'X': X, 'A': A, 'Wv': Wv, 'bv': bv, 'aw': aw, 'ab': ab, 'Wk': Wk, 'bk': bk}
    _L0_gnn_all = _L0_gnn_setup()
    _L0_gnn_in = {k: v for k, v in _L0_gnn_all.items() if k in ('Wv', 'bv', 'aw', 'ab', 'Wk', 'bk')}
    del _L0_gnn_all

    def _L1_gnn_setup():
        import jax, jax.numpy as jnp
        import numpy as np
        EPS = 1e-06
        key = jax.random.key(seed)
        k1, k2, k3 = jax.random.split(key, 3)
        B, N, F, O = (8, 2048, 256, 256)
        x = jax.random.normal(k1, (B, N, F), dtype=jnp.float32)
        adj = jax.random.uniform(k2, (B, N, N), dtype=jnp.float32)
        W = jax.random.normal(k3, (O, 2 * F), dtype=jnp.float32) * (1.0 / np.sqrt(2 * F))
        return {'x': x, 'adj': adj, 'W': W}
    _L1_gnn_all = _L1_gnn_setup()
    _L1_gnn_in = {k: v for k, v in _L1_gnn_all.items() if k in ('W',)}
    del _L1_gnn_all
    return {'x': x, 'adj': adj, 'L0_gnn_Wv': _L0_gnn_in['Wv'], 'L0_gnn_bv': _L0_gnn_in['bv'], 'L0_gnn_aw': _L0_gnn_in['aw'], 'L0_gnn_ab': _L0_gnn_in['ab'], 'L0_gnn_Wk': _L0_gnn_in['Wk'], 'L0_gnn_bk': _L0_gnn_in['bk'], 'L1_gnn_W': _L1_gnn_in['W']}

def reference(x, adj, L0_gnn_Wv, L0_gnn_bv, L0_gnn_aw, L0_gnn_ab, L0_gnn_Wk, L0_gnn_bk, L1_gnn_W):
    import jax
    import jax.numpy as jnp

    def _L0_gnn_ref(X, A, Wv, bv, aw, ab, Wk, bk):
        import jax, jax.numpy as jnp
        import numpy as np
        B, N, DIN, DOUT, K = (4, 1024, 256, 256, 3)
        d = Wv.shape[1]
        Xw = X @ Wv + bv
        sj = Xw @ aw[:d, 0]
        si = Xw @ aw[d:, 0]
        e = jax.nn.leaky_relu(sj[:, None, :] + si[:, :, None] + ab[0], negative_slope=0.2)
        alpha_matrix = A * jnp.exp(e)
        transition = alpha_matrix / (jnp.sum(alpha_matrix, axis=-1, keepdims=True) + 1e-12)
        H = jnp.zeros(X.shape[:-1] + (d,), dtype=X.dtype)
        Xk = X
        for k in range(Wk.shape[0]):
            H = H + Xk @ Wk[k] + bk[k]
            Xk = jnp.einsum('bij,bjd->bid', transition, Xk)
        return jax.nn.relu(H)

    def _L1_gnn_ref(x, adj, W):
        import jax, jax.numpy as jnp
        import numpy as np
        EPS = 1e-06
        deg = jnp.sum(adj, axis=-1, keepdims=True)
        agg = jnp.einsum('bij,bjf->bif', adj, x) / jnp.maximum(deg, EPS)
        cat = jnp.concatenate([x, agg], axis=2)
        out = jnp.einsum('bnf,of->bno', cat, W)
        return jax.nn.relu(out)
    x = _layernorm(x + _L0_gnn_ref(x, adj, L0_gnn_Wv, L0_gnn_bv, L0_gnn_aw, L0_gnn_ab, L0_gnn_Wk, L0_gnn_bk), axis=-1)
    x = _layernorm(x + _L1_gnn_ref(x, adj, L1_gnn_W), axis=-1)
    return x

_drawn_inputs = setup_inputs


def setup_inputs(seed=0):
    import zlib

    import numpy as np

    out = dict(_drawn_inputs(seed))
    spreads = {}
    factors = {'L0_gnn_Wv': 4.412, 'L0_gnn_bv': 23.531, 'L0_gnn_aw': 4.499}
    for name, (base, spread) in spreads.items():
        noise = np.random.default_rng([zlib.crc32(name.encode()), seed]).standard_normal(out[name].shape)
        drawn = base * np.exp(spread * noise) if base else spread * noise
        out[name] = jnp.asarray(drawn.astype(out[name].dtype))
    for name, factor in factors.items():
        out[name] = (out[name] * factor).astype(out[name].dtype)
    return out
```

```python
from contextlib import ExitStack

import concourse.bass as bass
from concourse import mybir

ALU = mybir.AluOpType
ACT = mybir.ActivationFunctionType
F32 = mybir.dt.float32
F32R = mybir.dt.float32r

P = 128
D = 256
C = D // P
GP = 2
LEAK = 0.2
LN_EPS = 1e-5
ROW_EPS = 1e-12
DEG_EPS = 1e-6


def wait_count(eng, sem, count):
    if not (isinstance(count, int) and count <= 0):
        eng.wait_ge(sem, count)


def graph_layers_kernel(nc, xt, adj, x, adjt, wk, wvt, aw, bv, ab, bk, w1, out):
    NP = xt.shape[0]
    LEAD, LAG = 3, 3
    LOOP0 = 6
    LOOP1 = NP - LEAD - (NP - LEAD) % 2

    def there(r):
        return not isinstance(r, int) or 0 <= r < NP

    def steps(eng, step):
        for p in range(-LEAD, LOOP0):
            step(p, p % 2)
        with eng.Fori(LOOP0, LOOP1, 2) as i:
            step(i, 0)
            step(i + 1, 1)
        for p in range(LOOP1, NP + LAG):
            step(p, p % 2)

    def dma_count(r, k):
        return (r - k) * 8 + 16

    with ExitStack() as ctx:
        def sb(name, shape, dt=F32):
            return ctx.enter_context(nc.sbuf_tensor(name, shape, dt))

        def psum(name, shape):
            return ctx.enter_context(nc.psum_tensor(name, shape, F32))

        def sem(name):
            return ctx.enter_context(nc.semaphore(name))

        def sem2(name):
            return [sem(f"{name}_0"), sem(f"{name}_1")]

        ps_m = psum("ps_m", [P, GP, 512])
        ps_z = psum("ps_z", [P, GP, 512])
        ps_q = psum("ps_q", [P, GP, 512])
        ps_x = psum("ps_x", [P, GP, C, P])
        ps_u = psum("ps_u", [P, 2, GP, P])

        ident = sb("ident", [P, P])
        ones = sb("ones", [P, P])
        ones_r = sb("ones_r", [P, P], F32R)
        half = sb("half", [P, GP])
        wk_raw = sb("wk_raw", [P, C, 3 * D])
        w1_raw = sb("w1_raw", [P, C, 2 * D])
        w01_hi = sb("w01_hi", [P, C, 2 * D], F32R)
        w01_lo = sb("w01_lo", [P, C, 2 * D], F32R)
        w2s_hi = sb("w2s_hi", [P, C, D + 2], F32R)
        w2s_lo = sb("w2s_lo", [P, C, D + 2], F32R)
        w1_hi = sb("w1_hi", [P, C, 2 * D], F32R)
        w1_lo = sb("w1_lo", [P, C, 2 * D], F32R)
        wvt_sb = sb("wvt_sb", [P, C, D])
        aw_sb = sb("aw_sb", [P, C, 2])
        bv_sb = sb("bv_sb", [P, C])
        ws = sb("ws", [P, C, 2])
        cprod = sb("cprod", [P, 4])
        chalf = sb("chalf", [P, 1])
        bk_raw = sb("bk_raw", [P, D])
        bias_r = sb("bias_r", [P, D], F32R)
        bias_t = sb("bias_t", [P, D], F32R)

        xt_raw = sb("xt_raw", [P, 2, GP * C * P])
        adj_sb = sb("adj_sb", [P, 2, GP * P])
        x_sb = sb("x_sb", [P, 2, GP * D])
        adjt_raw = sb("adjt_raw", [P, 2, GP * P])

        xt_hi = sb("xt_hi", [P, 2, GP * C * P], F32R)
        xt_lo = sb("xt_lo", [P, 2, GP * C * P], F32R)
        xw2_hi = sb("xw2_hi", [P, 2, GP, D], F32R)
        xw2_lo = sb("xw2_lo", [P, 2, GP, D], F32R)
        score = sb("score", [P, GP, 2])
        e_sum = sb("e_sum", [P, GP, P])
        e_leaky = sb("e_leaky", [P, GP * P])
        e_exp = sb("e_exp", [P, GP, P])
        alpha = sb("alpha", [P, GP, P])
        rowsum = sb("rowsum", [P, GP])
        rowsum_e = sb("rowsum_e", [P, GP])
        rowinv = sb("rowinv", [P, GP])
        trans = sb("trans", [P, GP, P])
        tt_hi = sb("tt_hi", [P, GP, P], F32R)
        tt_lo = sb("tt_lo", [P, GP, P], F32R)
        z_hi = sb("z_hi", [P, GP, D], F32R)
        z_lo = sb("z_lo", [P, GP, D], F32R)
        y1 = sb("y1", [P, GP, D])
        bn6 = sb("bn6", [P, GP, 6])
        mv = sb("mv", [P, GP, 2])
        var1 = sb("var1", [P, GP])
        rstd1 = sb("rstd1", [P, GP])
        x1 = sb("x1", [P, 2, GP, D])
        x1t_hi = sb("x1t_hi", [P, GP, C, P], F32R)
        x1t_lo = sb("x1t_lo", [P, GP, C, P], F32R)
        adjt_hi = sb("adjt_hi", [P, 2, GP * P], F32R)
        adjt_lo = sb("adjt_lo", [P, 2, GP * P], F32R)
        self_sb = sb("self_sb", [P, GP, D])
        q_hi = sb("q_hi", [P, GP, D + 2], F32R)
        q_lo = sb("q_lo", [P, GP, D], F32R)
        deg = sb("deg", [P, GP])
        deginv = sb("deginv", [P, GP])
        o_sum = sb("o_sum", [P, GP, D])
        y2 = sb("y2", [P, 2, GP, D])
        sum2 = sb("sum2", [P, 2, GP])
        nmean2 = sb("nmean2", [P, 2, GP])
        sq_out = sb("sq_out", [P, GP, D])
        sq2 = sb("sq2", [P, 2, GP])
        var2 = sb("var2", [P, 2, GP])
        rstd2 = sb("rstd2", [P, 2, GP])
        shift2 = sb("shift2", [P, 2, GP])
        out_sb = sb("out_sb", [P, 2, GP, D])

        s_w = sem("weights_loaded")
        s_zero = sem("bias_rows_zeroed")
        s_bk = sem("bias_rows_loaded")
        s_fill = sem("ident_filled")
        s_id = sem("ident_ready")
        s_const = sem("consts_ready")
        s_ws = sem("score_weights_in_psum")
        s_cp = sem("score_const_products")
        s_cs = sem("score_const_in_psum")
        s_dset = sem("dve_setup_chain")
        s_wready = sem("weights_split")
        xt_in, adj_in, x_in, adjt_in = sem2("xt_in"), sem2("adj_in"), sem2("x_in"), sem2("adjt_in")
        stored = sem2("out_stored")
        s_xt_hi, s_xt_lo, s_xt_used = sem("xt_hi_ready"), sem("xt_lo_ready"), sem("xt_used")
        s_xw2 = sem2("xw2_in_psum")
        s_xw2_hi, s_xw2_lo = sem2("xw2_hi_ready"), sem2("xw2_lo_ready")
        s_score = sem("score_ready")
        s_u = sem("src_score_in_psum")
        s_esum, s_leaky, s_exp = sem("e_sum_ready"), sem("e_leaky_ready"), sem("e_exp_ready")
        s_alpha, s_rowe, s_rowinv, s_trans = sem("alpha_ready"), sem("rowsum_e_ready"), sem("rowinv_ready"), sem("trans_ready")
        s_tt, s_tt_hi, s_tt_lo = sem("tt_in_psum"), sem("tt_hi_ready"), sem("tt_lo_ready")
        s_z, s_z_hi, s_z_lo = sem2("z_in_psum"), sem2("z_hi_ready"), sem2("z_lo_ready")
        s_h = sem2("h_in_psum")
        s_y1 = sem2("y1_ready")
        s_bn, s_mv, s_var1 = sem2("y1_stats"), sem2("mv_ready"), sem("var1_ready")
        s_rstd1 = sem("rstd1_ready")
        s_x1 = sem2("x1_ready")
        s_x1t, s_x1t_hi, s_x1t_lo = sem("x1t_in_psum"), sem("x1t_hi_ready"), sem("x1t_lo_ready")
        s_adjt_hi, s_adjt_lo = sem("adjt_hi_ready"), sem("adjt_lo_ready")
        s_pq, s_q_hi, s_q_lo, s_self = sem2("x1w_in_psum"), sem2("q_hi_ready"), sem2("q_lo_ready"), sem2("self_ready")
        s_agg = sem2("agg_in_psum")
        s_deg, s_deginv = sem("deg_ready"), sem("deginv_ready")
        s_o = sem2("o_sum_ready")
        s_y2, s_nmean2, s_sq2, s_var2 = sem2("y2_ready"), sem("nmean2_ready"), sem2("sq2_ready"), sem("var2_ready")
        s_rstd2, s_shift2, s_out = sem("rstd2_ready"), sem("shift2_ready"), sem("out_ready")

        N_SETUP_LOADS = 6

        block = ctx.enter_context(nc.Block())

        @block.sync
        def _(sp):
            sp.dma_start(wk_raw[:], wk).then_inc(s_w, 16)
            sp.dma_start(wvt_sb[:], wvt).then_inc(s_w, 16)
            sp.dma_start(aw_sb[:], aw).then_inc(s_w, 16)
            sp.dma_start(bv_sb[:], bv).then_inc(s_w, 16)
            sp.dma_start(w1_raw[:], w1).then_inc(s_w, 16)
            sp.wait_ge(s_zero, 2)
            sp.dma_start(cprod[0:1, 2:3], ab).then_inc(s_w, 16)
            sp.dma_start(bk_raw[0:3, :], bk).then_inc(s_bk, 16)
            sp.dma_start(bk_raw[32:35, :], bk).then_inc(s_bk, 16)

            def load_xt(r, k):
                wait_count(sp, s_xt_hi, r - 1)
                wait_count(sp, s_xt_lo, r - 1)
                sp.dma_start(xt_raw[:, k, :], xt[r]).then_inc(xt_in[k], 16)

            def load_adj(r, k):
                wait_count(sp, s_alpha, r - 1)
                sp.dma_start(adj_sb[:, k, :], adj[r]).then_inc(adj_in[k], 16)

            def load_x(r, k):
                wait_count(sp, s_y1[1], r - 1)
                sp.dma_start(x_sb[:, k, :], x[r]).then_inc(x_in[k], 16)

            def load_adjt(r, k):
                wait_count(sp, s_adjt_hi, r - 1)
                wait_count(sp, s_adjt_lo, r - 1)
                sp.dma_start(adjt_raw[:, k, :], adjt[r]).then_inc(adjt_in[k], 16)

            def store(r, k):
                sp.wait_ge(s_out, r + 1)
                sp.dma_start(out[r], out_sb[:, k, :, :].rearrange("p g d -> p (g d)")).then_inc(stored[k], 16)

            def step(p, k):
                if there(p + 3):
                    load_xt(p + 3, 1 - k)
                if there(p + 2):
                    load_adj(p + 2, k)
                if there(p):
                    load_adjt(p, k)
                if there(p + 1):
                    load_x(p + 1, 1 - k)
                if there(p - 3):
                    store(p - 3, 1 - k)

            steps(sp, step)
            for k in range(2):
                sp.wait_ge(stored[k], 16 * ((NP + 1 - k) // 2))

        @block.tensor
        def _(pe):
            pe.wait_ge(s_w, 16 * N_SETUP_LOADS)
            for c in range(C):
                for k in range(C):
                    mm = nc.tensor.matmul(ps_m[:, 0, 2 * c:2 * c + 2], wvt_sb[:, k, c * P:(c + 1) * P],
                                          aw_sb[:, k, :], start=(k == 0), stop=(k == C - 1))
            mm.then_inc(s_ws, 1)
            pe.wait_ge(s_const, 1)
            pe.wait_ge(s_cp, 1)
            nc.tensor.matmul(ps_m[:, 1, 0:3], ones[:, :], cprod[:, 0:3], start=True, stop=True).then_inc(s_cs, 1)
            pe.wait_ge(s_wready, 1)
            pe.wait_ge(s_id, 1)

            def halves(acc, st_hi, st_lo, mv_hi, mv_lo, start, stop, wide=None):
                nc.tensor.matmul(acc(mv_hi), st_hi, mv_hi, start=start, stop=False, skip_group_check=True)
                nc.tensor.matmul(acc(mv_lo), st_hi, mv_lo, start=False, stop=False, skip_group_check=True)
                return nc.tensor.matmul(acc(mv_hi), st_lo, mv_hi, start=False, stop=stop, skip_group_check=True)

            def project2(r, k):
                pe.wait_ge(s_xt_hi, r + 1)
                pe.wait_ge(s_xt_lo, r + 1)
                for g in range(GP):
                    wait_count(pe, s_xw2_lo[g], r)
                    for c in range(C):
                        cols = slice((g * C + c) * P, (g * C + c + 1) * P)
                        mm = halves(lambda m: ps_m[:, g, 0:m.shape[-1]], xt_hi[:, k, cols], xt_lo[:, k, cols],
                                    w2s_hi[:, c, :], w2s_lo[:, c, :], c == 0, c == C - 1)
                    mm.then_inc(s_xw2[g], 1)

            def project01(r, k):
                for g in range(GP):
                    wait_count(pe, s_y1[g], r)
                    for c in range(C):
                        cols = slice((g * C + c) * P, (g * C + c + 1) * P)
                        mm = halves(lambda m: ps_z[:, g, 0:m.shape[-1]], xt_hi[:, k, cols], xt_lo[:, k, cols],
                                    w01_hi[:, c, :], w01_lo[:, c, :], c == 0, False)
                mm.then_inc(s_xt_used, 1)

            def spread_source(r):
                pe.wait_ge(s_score, r + 1)
                wait_count(pe, s_tt_lo, r)
                for g in range(GP):
                    mm = nc.tensor.transpose(ps_u[:, 0, g, :], score[:, g, 0:1].to_broadcast([P, P]), ident[:, :])
                mm.then_inc(s_u, 1)

            def transpose_t(r):
                pe.wait_ge(s_trans, r + 1)
                for g in range(GP):
                    mm = nc.tensor.transpose(ps_u[:, 1, g, :], trans[:, g, :], ident[:, :])
                mm.then_inc(s_tt, 1)

            def hop1(r, k):
                pe.wait_ge(s_tt_hi, r + 1)
                pe.wait_ge(s_tt_lo, r + 1)
                for g in range(GP):
                    pe.wait_ge(s_xw2_hi[g], r + 1)
                    pe.wait_ge(s_xw2_lo[g], r + 1)
                    halves(lambda m: ps_z[:, g, D:2 * D], tt_hi[:, g, :], tt_lo[:, g, :],
                           xw2_hi[:, k, g, :], xw2_lo[:, k, g, :], False, False).then_inc(s_z[g], 1)

            def hop2(r):
                for g in range(GP):
                    pe.wait_ge(s_z_hi[g], r + 1)
                    pe.wait_ge(s_z_lo[g], r + 1)
                    nc.tensor.matmul(ps_z[:, g, 0:D], ones_r[:, :], bias_r[:, :], start=False, stop=False,
                                     skip_group_check=True)
                    halves(lambda m: ps_z[:, g, 0:D], tt_hi[:, g, :], tt_lo[:, g, :],
                           z_hi[:, g, :], z_lo[:, g, :], False, True).then_inc(s_h[g], 1)

            def transpose_x1(r, k):
                wait_count(pe, s_x1t_lo, r)
                for g in range(GP):
                    pe.wait_ge(s_x1[g], r + 1)
                    for c in range(C):
                        mm = nc.tensor.transpose(ps_x[:, g, c, :], x1[:, k, g, c * P:(c + 1) * P], ident[:, :])
                mm.then_inc(s_x1t, 1)

            def project_x1(r):
                pe.wait_ge(s_x1t_hi, r + 1)
                for g in range(GP):
                    wait_count(pe, s_o[g], r)
                    for c in range(C):
                        nc.tensor.matmul(ps_q[:, g, :], x1t_hi[:, g, c, :], w1_hi[:, c, :], start=(c == 0),
                                         stop=False, skip_group_check=True)
                        nc.tensor.matmul(ps_q[:, g, :], x1t_hi[:, g, c, :], w1_lo[:, c, :], start=False,
                                         stop=False, skip_group_check=True)
                    if g == 0:
                        pe.wait_ge(s_x1t_lo, r + 1)
                    for c in range(C):
                        mm = nc.tensor.matmul(ps_q[:, g, :], x1t_lo[:, g, c, :], w1_hi[:, c, :], start=False,
                                              stop=(c == C - 1), skip_group_check=True)
                    mm.then_inc(s_pq[g], 1)

            def aggregate(r, k):
                pe.wait_ge(s_adjt_hi, r + 1)
                pe.wait_ge(s_adjt_lo, r + 1)
                for g in range(GP):
                    pe.wait_ge(s_self[g], r + 1)
                    pe.wait_ge(s_q_hi[g], r + 1)
                    pe.wait_ge(s_q_lo[g], r + 1)
                    cols = slice(g * P, (g + 1) * P)
                    halves(lambda m: ps_q[:, g, 0:m.shape[-1]], adjt_hi[:, k, cols], adjt_lo[:, k, cols],
                           q_hi[:, g, :], q_lo[:, g, :], True, True).then_inc(s_agg[g], 1)

            def step(p, k):
                if there(p + 1):
                    project2(p + 1, 1 - k)
                if there(p - 2):
                    aggregate(p - 2, k)
                if there(p):
                    transpose_t(p)
                    project01(p, k)
                if there(p - 1):
                    transpose_x1(p - 1, 1 - k)
                if there(p):
                    hop1(p, k)
                if there(p + 1):
                    spread_source(p + 1)
                if there(p - 1):
                    project_x1(p - 1)
                if there(p):
                    hop2(p)

            steps(pe, step)

        @block.scalar
        def _(act):
            def copy_score(r):
                act.wait_ge(s_xw2[0], r + 1)
                act.wait_ge(s_xw2[1], r + 1)
                wait_count(act, s_u, r)
                nc.scalar.activation(score[:, :, :], ps_m[:, :, D:D + 2], ACT.Identity,
                                     bias=chalf[:, 0:1]).then_inc(s_score, 1)

            def split_xw2(r, k, g):
                wait_count(act, s_z[g], r - 1)
                nc.scalar.activation(xw2_hi[:, k, g, :], ps_m[:, g, 0:D], ACT.Copy).then_inc(s_xw2_hi[g], 1)

            def split_tt(r):
                act.wait_ge(s_tt, r + 1)
                wait_count(act, s_h[1], r)
                nc.scalar.activation(tt_hi[:, :, :], ps_u[:, 1, :, :], ACT.Copy).then_inc(s_tt_hi, 1)

            def split_adjt(r, k):
                act.wait_ge(adjt_in[k], dma_count(r, k))
                wait_count(act, s_agg[1], r - 1)
                nc.scalar.activation(adjt_hi[:, k, :], adjt_raw[:, k, :], ACT.Copy).then_inc(s_adjt_hi, 1)

            def split_x1t(r):
                act.wait_ge(s_x1t, r + 1)
                wait_count(act, s_pq[1], r)
                nc.scalar.activation(x1t_hi[:, :, :, :], ps_x[:, :, :, :], ACT.Copy).then_inc(s_x1t_hi, 1)

            def add_scores(r):
                act.wait_ge(s_u, r + 1)
                act.wait_ge(s_score, r + 1)
                wait_count(act, s_leaky, r)
                for g in range(GP):
                    a = nc.scalar.activation(e_sum[:, g, :], ps_u[:, 0, g, :], ACT.Identity,
                                             bias=score[:, g, 1:2])
                a.then_inc(s_esum, 1)

            def split_z(r, g):
                act.wait_ge(s_z[g], r + 1)
                wait_count(act, s_h[g], r)
                nc.scalar.activation(z_hi[:, g, :], ps_z[:, g, D:2 * D], ACT.Copy).then_inc(s_z_hi[g], 1)

            def square_y2(r, k):
                act.wait_ge(s_nmean2, r + 1)
                wait_count(act, s_var2, r - 1)
                for g in range(GP):
                    nc.scalar.activation(sq_out[:, g, :], y2[:, k, g, :], ACT.Square, bias=nmean2[:, k, g:g + 1],
                                         accum_out=sq2[:, k, g:g + 1]).then_inc(s_sq2[g], 1)

            def split_xt(r, k):
                act.wait_ge(xt_in[k], dma_count(r, k))
                wait_count(act, s_xt_used, r - 1)
                nc.scalar.activation(xt_hi[:, k, :], xt_raw[:, k, :], ACT.Copy).then_inc(s_xt_hi, 1)

            def exponential(r):
                act.wait_ge(s_leaky, r + 1)
                wait_count(act, s_alpha, r)
                nc.scalar.activation(e_exp[:, :, :], e_leaky[:, :].rearrange("p (g n) -> p g n", g=GP),
                                     ACT.Exp).then_inc(s_exp, 1)

            def split_q(r, g):
                act.wait_ge(s_pq[g], r + 1)
                wait_count(act, s_o[g], r)
                nc.scalar.activation(self_sb[:, g, :], ps_q[:, g, 0:D], ACT.Copy).then_inc(s_self[g], 1)
                wait_count(act, s_agg[g], r)
                nc.scalar.activation(q_hi[:, g, 0:D], ps_q[:, g, D:2 * D], ACT.Copy).then_inc(s_q_hi[g], 1)

            def scale_rows(r):
                act.wait_ge(s_rowinv, r + 1)
                wait_count(act, s_tt, r)
                for g in range(GP):
                    a = nc.scalar.activation(trans[:, g, :], alpha[:, g, :], ACT.Copy, scale=rowinv[:, g:g + 1])
                a.then_inc(s_trans, 1)

            act.wait_ge(s_wready, 1)

            def step(p, k):
                if there(p + 1):
                    copy_score(p + 1)
                    split_xw2(p + 1, 1 - k, 0)
                    split_xw2(p + 1, 1 - k, 1)
                if there(p):
                    split_tt(p)
                if there(p - 1):
                    split_adjt(p - 1, 1 - k)
                    split_x1t(p - 1)
                if there(p + 1):
                    add_scores(p + 1)
                if there(p):
                    split_z(p, 0)
                    split_z(p, 1)
                if there(p - 2):
                    square_y2(p - 2, k)
                if there(p + 2):
                    split_xt(p + 2, k)
                if there(p + 1):
                    exponential(p + 1)
                if there(p - 1):
                    split_q(p - 1, 0)
                if there(p + 1):
                    scale_rows(p + 1)
                if there(p - 1):
                    split_q(p - 1, 1)

            steps(act, step)

        @block.gpsimd
        def _(pool):
            nc.gpsimd.memset(cprod[:], 0.0).then_inc(s_zero, 1)
            nc.gpsimd.memset(bk_raw[:], 0.0).then_inc(s_zero, 1)
            nc.gpsimd.memset(ident[:], 0.0).then_inc(s_fill, 1)
            nc.gpsimd.memset(half[:], -0.5).then_inc(s_fill, 1)
            pool.wait_ge(s_fill, 2)
            nc.gpsimd.affine_select(out=ident[:], in_=ident[:], compare_op=ALU.not_equal, fill=1.0, base=0,
                                    pattern=[[-1, P]], channel_multiplier=1).then_inc(s_id, 1)

            def rstd_of_y1(r):
                pool.wait_ge(s_var1, r + 1)
                wait_count(pool, s_x1[1], r)
                nc.gpsimd.tensor_tensor(rstd1[:, :], var1[:, :], half[:, :], ALU.pow).then_inc(s_rstd1, 1)

            def split_adjt(r, k):
                pool.wait_ge(s_adjt_hi, r + 1)
                wait_count(pool, s_agg[1], r - 1)
                nc.gpsimd.tensor_tensor(adjt_lo[:, k, :], adjt_raw[:, k, :], adjt_hi[:, k, :].bitcast(F32),
                                        ALU.subtract).then_inc(s_adjt_lo, 1)

            def y2_scale_ready(r, k):
                wait_count(pool, stored[k], dma_count(r - 2, k))
                pool.wait_ge(s_shift2, r + 1)

            def normalise_y2(r, k):
                for g in range(GP):
                    t = nc.gpsimd.tensor_scalar(out_sb[:, k, g, :], y2[:, k, g, :], rstd2[:, k, g:g + 1],
                                                shift2[:, k, g:g + 1], ALU.mult, ALU.add)
                t.then_inc(s_out, 1)

            def split_xt(r, k):
                pool.wait_ge(s_xt_hi, r + 1)
                wait_count(pool, s_xt_used, r - 1)
                nc.gpsimd.tensor_tensor(xt_lo[:, k, :], xt_raw[:, k, :], xt_hi[:, k, :].bitcast(F32),
                                        ALU.subtract).then_inc(s_xt_lo, 1)

            def rstd_of_y2(r, k):
                pool.wait_ge(s_var2, r + 1)
                nc.gpsimd.tensor_tensor(rstd2[:, k, :], var2[:, k, :], half[:, :], ALU.pow).then_inc(s_rstd2, 1)
                pool.wait_ge(s_rstd2, r + 1)
                nc.gpsimd.tensor_tensor(shift2[:, k, :], rstd2[:, k, :], nmean2[:, k, :],
                                        ALU.mult).then_inc(s_shift2, 1)

            def step(p, k):
                if there(p - 3):
                    y2_scale_ready(p - 3, 1 - k)
                if there(p - 1):
                    rstd_of_y1(p - 1)
                if there(p - 3):
                    normalise_y2(p - 3, 1 - k)
                if there(p - 1):
                    split_adjt(p - 1, 1 - k)
                if there(p + 2):
                    split_xt(p + 2, k)
                if there(p - 2):
                    rstd_of_y2(p - 2, k)

            steps(pool, step)

        @block.vector
        def _(dve):
            links = [0]

            def link(ins):
                links[0] += 1
                ins.then_inc(s_dset, 1)
                dve.wait_ge(s_dset, links[0])

            nc.vector.memset(ones[:], 1.0).then_inc(s_const, 1)
            dve.wait_ge(s_const, 1)
            link(nc.vector.tensor_copy(ones_r[:], ones[:]))
            for g in range(GP):
                link(nc.vector.tensor_copy(q_hi[:, g, D:D + 2], ones[:, 0:2]))
            dve.wait_ge(s_w, 16 * N_SETUP_LOADS)
            link(nc.vector.tensor_tensor(cprod[:, 0:C], aw_sb[:, :, 0], aw_sb[:, :, 1], ALU.add))
            nc.vector.tensor_tensor(cprod[:, 0:C], cprod[:, 0:C], bv_sb[:, :], ALU.mult).then_inc(s_cp, 1)
            for hi, lo, raw in ((w01_hi, w01_lo, wk_raw[:, :, 0:2 * D]), (w1_hi, w1_lo, w1_raw[:, :, :])):
                link(nc.vector.tensor_copy(hi[:, :, :], raw))
                link(nc.vector.tensor_tensor(lo[:, :, :], raw, hi[:, :, :].bitcast(F32), ALU.subtract))
            link(nc.vector.tensor_copy(w2s_hi[:, :, 0:D], wk_raw[:, :, 2 * D:3 * D]))
            link(nc.vector.tensor_tensor(w2s_lo[:, :, 0:D], wk_raw[:, :, 2 * D:3 * D],
                                         w2s_hi[:, :, 0:D].bitcast(F32), ALU.subtract))
            dve.wait_ge(s_ws, 1)
            link(nc.vector.tensor_copy(ws[:, :, :], ps_m[:, 0, 0:2 * C].rearrange("p (c s) -> p c s", c=C)))
            link(nc.vector.tensor_copy(w2s_hi[:, :, D:D + 2], ws[:, :, :]))
            link(nc.vector.tensor_tensor(w2s_lo[:, :, D:D + 2], ws[:, :, :],
                                         w2s_hi[:, :, D:D + 2].bitcast(F32), ALU.subtract))
            dve.wait_ge(s_cs, 1)
            link(nc.vector.reduce_sum(chalf[:, :], ps_m[:, 1, 0:3], axis=mybir.AxisListType.X))
            link(nc.vector.tensor_scalar(chalf[:, :], chalf[:, :], 0.5, None, ALU.mult))
            dve.wait_ge(s_bk, 32)
            link(nc.vector.tensor_copy(bias_t[:, :], bk_raw[:, :]))
            link(nc.vector.tensor_tensor(bias_r[:, :], bk_raw[:, :], bias_t[:, :].bitcast(F32), ALU.subtract))
            nc.vector.tensor_copy(bias_r[0:32, :], bk_raw[0:32, :]).then_inc(s_wready, 1)

            def residual1(r, k):
                dve.wait_ge(x_in[k], dma_count(r, k))
                for g in range(GP):
                    dve.wait_ge(s_h[g], r + 1)
                    nc.vector.scalar_tensor_tensor(out=y1[:, g, :], in0=ps_z[:, g, 0:D], scalar=0.0,
                                                   in1=x_sb[:, k, g * D:(g + 1) * D], op0=ALU.max,
                                                   op1=ALU.add).then_inc(s_y1[g], 1)

            def statistics1(r):
                for g in range(GP):
                    dve.wait_ge(s_y1[g], r + 1)
                    nc.vector.bn_stats(bn6[:, g, :], y1[:, g, :]).then_inc(s_bn[g], 1)

            def stats1_written(r):
                dve.wait_ge(s_bn[0], r + 1)
                dve.wait_ge(s_bn[1], r + 1)

            def moments1(r):
                for g in range(GP):
                    nc.vector.bn_aggr(mv[:, g, :], bn6[:, g, :]).then_inc(s_mv[g], 1)
                dve.wait_ge(s_mv[0], r + 1)
                dve.wait_ge(s_mv[1], r + 1)
                wait_count(dve, s_rstd1, r)
                nc.vector.tensor_scalar(var1[:, :], mv[:, :, 1], LN_EPS, None, ALU.add).then_inc(s_var1, 1)

            def split_xw2(r, k, g):
                dve.wait_ge(s_score, r + 1)
                dve.wait_ge(s_xw2_hi[g], r + 1)
                wait_count(dve, s_z[g], r - 1)
                nc.vector.tensor_tensor(xw2_lo[:, k, g, :], ps_m[:, g, 0:D], xw2_hi[:, k, g, :].bitcast(F32),
                                        ALU.subtract).then_inc(s_xw2_lo[g], 1)

            def split_tt(r):
                dve.wait_ge(s_tt_hi, r + 1)
                wait_count(dve, s_h[1], r)
                nc.vector.tensor_tensor(tt_lo[:, :, :], ps_u[:, 1, :, :], tt_hi[:, :, :].bitcast(F32),
                                        ALU.subtract).then_inc(s_tt_lo, 1)

            def normalise_y1(r, k):
                dve.wait_ge(s_rstd1, r + 1)
                wait_count(dve, s_x1t, r - 1)
                for g in range(GP):
                    nc.vector.tensor_scalar(x1[:, k, g, :], y1[:, g, :], mv[:, g, 0:1], rstd1[:, g:g + 1],
                                            ALU.subtract, ALU.mult).then_inc(s_x1[g], 1)

            def residual2(r, k):
                dve.wait_ge(s_agg[0], r + 1)
                dve.wait_ge(s_agg[1], r + 1)
                nc.vector.tensor_scalar(deg[:, :], ps_q[:, :, D], DEG_EPS, None, ALU.max).then_inc(s_deg, 1)
                dve.wait_ge(s_deg, r + 1)
                nc.vector.reciprocal(deginv[:, :], deg[:, :]).then_inc(s_deginv, 1)
                dve.wait_ge(s_deginv, r + 1)
                for g in range(GP):
                    dve.wait_ge(s_self[g], r + 1)
                    nc.vector.scalar_tensor_tensor(out=o_sum[:, g, :], in0=ps_q[:, g, 0:D],
                                                   scalar=deginv[:, g:g + 1], in1=self_sb[:, g, :],
                                                   op0=ALU.mult, op1=ALU.add).then_inc(s_o[g], 1)
                wait_count(dve, s_out, r - 1)
                wait_count(dve, s_sq2[1], r - 1)
                for g in range(GP):
                    dve.wait_ge(s_o[g], r + 1)
                    nc.vector.scalar_tensor_tensor(out=y2[:, k, g, :], in0=o_sum[:, g, :], scalar=0.0,
                                                   in1=x1[:, k, g, :], op0=ALU.max, op1=ALU.add,
                                                   accum_out=sum2[:, k, g:g + 1]).then_inc(s_y2[g], 1)

            def mean2(r, k):
                dve.wait_ge(s_y2[0], r + 1)
                dve.wait_ge(s_y2[1], r + 1)
                wait_count(dve, s_shift2, r - 1)
                nc.vector.tensor_scalar(nmean2[:, k, :], sum2[:, k, :], -1.0 / D, None,
                                        ALU.mult).then_inc(s_nmean2, 1)

            def split_x1t(r):
                dve.wait_ge(s_x1t_hi, r + 1)
                wait_count(dve, s_pq[1], r)
                nc.vector.tensor_tensor(x1t_lo[:, :, :, :], ps_x[:, :, :, :], x1t_hi[:, :, :, :].bitcast(F32),
                                        ALU.subtract).then_inc(s_x1t_lo, 1)

            def leaky(r):
                dve.wait_ge(s_esum, r + 1)
                wait_count(dve, s_exp, r)
                e = e_sum[:, :, :].rearrange("p g n -> p (g n)")
                nc.vector.scalar_tensor_tensor(out=e_leaky[:, :], in0=e, scalar=LEAK, in1=e, op0=ALU.mult,
                                               op1=ALU.max).then_inc(s_leaky, 1)

            def split_z(r, g):
                dve.wait_ge(s_z_hi[g], r + 1)
                wait_count(dve, s_h[g], r)
                nc.vector.tensor_tensor(z_lo[:, g, :], ps_z[:, g, D:2 * D], z_hi[:, g, :].bitcast(F32),
                                        ALU.subtract).then_inc(s_z_lo[g], 1)

            def weigh(r, k):
                dve.wait_ge(adj_in[k], dma_count(r, k))
                dve.wait_ge(s_exp, r + 1)
                wait_count(dve, s_trans, r)
                for g in range(GP):
                    a = nc.vector.tensor_tensor_reduce(alpha[:, g, :], adj_sb[:, k, g * P:(g + 1) * P],
                                                       e_exp[:, g, :], 1.0, 0.0, ALU.mult, ALU.add,
                                                       rowsum[:, g:g + 1])
                a.then_inc(s_alpha, 1)
                dve.wait_ge(s_alpha, r + 1)
                nc.vector.tensor_scalar(rowsum_e[:, :], rowsum[:, :], ROW_EPS, None, ALU.add).then_inc(s_rowe, 1)
                dve.wait_ge(s_rowe, r + 1)
                nc.vector.reciprocal(rowinv[:, :], rowsum_e[:, :]).then_inc(s_rowinv, 1)

            def variance2(r, k):
                dve.wait_ge(s_sq2[0], r + 1)
                dve.wait_ge(s_sq2[1], r + 1)
                wait_count(dve, s_rstd2, r - 1)
                nc.vector.tensor_scalar(var2[:, k, :], sq2[:, k, :], 1.0 / D, LN_EPS, ALU.mult,
                                        ALU.add).then_inc(s_var2, 1)

            def split_q(r, g):
                dve.wait_ge(s_q_hi[g], r + 1)
                wait_count(dve, s_agg[g], r)
                nc.vector.tensor_tensor(q_lo[:, g, :], ps_q[:, g, D:2 * D], q_hi[:, g, 0:D].bitcast(F32),
                                        ALU.subtract).then_inc(s_q_lo[g], 1)

            def step(p, k):
                if there(p - 1):
                    residual1(p - 1, 1 - k)
                    statistics1(p - 1)
                    stats1_written(p - 1)
                if there(p + 1):
                    split_xw2(p + 1, 1 - k, 0)
                if there(p - 1):
                    moments1(p - 1)
                if there(p + 1):
                    split_xw2(p + 1, 1 - k, 1)
                if there(p):
                    split_tt(p)
                if there(p - 1):
                    normalise_y1(p - 1, 1 - k)
                if there(p - 2):
                    residual2(p - 2, k)
                    mean2(p - 2, k)
                if there(p - 1):
                    split_x1t(p - 1)
                if there(p + 1):
                    leaky(p + 1)
                if there(p):
                    split_z(p, 0)
                    split_z(p, 1)
                if there(p + 1):
                    weigh(p + 1, 1 - k)
                if there(p - 2):
                    variance2(p - 2, k)
                if there(p - 1):
                    split_q(p - 1, 0)
                    split_q(p - 1, 1)

            steps(dve, step)


def kernel(x, adj, L0_gnn_Wv, L0_gnn_bv, L0_gnn_aw, L0_gnn_ab, L0_gnn_Wk, L0_gnn_bk, L1_gnn_W):
    import numpy as np
    import concourse.bacc as bacc
    from concourse.bass_utils import run_bass_kernel_spmd

    x, adj = np.asarray(x), np.asarray(adj)
    Wv, bv, aw, ab = (np.asarray(a) for a in (L0_gnn_Wv, L0_gnn_bv, L0_gnn_aw, L0_gnn_ab))
    Wk, bk, W1 = np.asarray(L0_gnn_Wk), np.asarray(L0_gnn_bk), np.asarray(L1_gnn_W)
    B = x.shape[0]
    NP = B // GP

    def rows(a):
        return a.reshape(C, P, -1).transpose(1, 0, 2)

    arrays = {
        "in_xt": x.reshape(NP, GP, P, C, P).transpose(0, 4, 1, 3, 2).reshape(NP, P, GP * C * P),
        "in_adj": adj.reshape(NP, GP, P, P).transpose(0, 2, 1, 3).reshape(NP, P, GP * P),
        "in_x": x.reshape(NP, GP, P, D).transpose(0, 2, 1, 3).reshape(NP, P, GP * D),
        "in_adjt": adj.reshape(NP, GP, P, P).transpose(0, 3, 1, 2).reshape(NP, P, GP * P),
        "in_wk": rows(Wk.transpose(1, 0, 2).reshape(D, 3 * D)),
        "in_wvt": rows(Wv.T),
        "in_aw": rows(aw.reshape(2, D).T),
        "in_bv": bv.reshape(C, P).T,
        "in_ab": ab.reshape(1, 1),
        "in_bk": bk,
        "in_w1": rows(W1.reshape(D, 2, D).transpose(2, 1, 0).reshape(D, 2 * D)),
    }
    arrays = {n: np.ascontiguousarray(a) for n, a in arrays.items()}
    nc = bacc.Bacc("TRN2", target_bir_lowering=False, num_devices=1)
    args = [nc.dram_tensor(n, a.shape, mybir.dt.from_np(a.dtype), kind="ExternalInput").ap()
            for n, a in arrays.items()]
    args.append(nc.dram_tensor("out_y", (NP, P, GP * D), F32, kind="ExternalOutput").ap())
    graph_layers_kernel(nc, *args)
    got = run_bass_kernel_spmd(nc, [arrays], core_ids=[0]).results[0]["out_y"]
    return got.reshape(NP, P, GP, D).transpose(0, 2, 1, 3).reshape(B, P, D)
```

```python
from contextlib import ExitStack

import concourse.bass as bass
from concourse import mybir

ALU = mybir.AluOpType
ACT = mybir.ActivationFunctionType
F32 = mybir.dt.float32
F32R = mybir.dt.float32r

P = 128
D = 256
C = D // P
GP = 2
LEAK = 0.2
LN_EPS = 1e-5
ROW_EPS = 1e-12
DEG_EPS = 1e-6


def wait_count(eng, sem, count):
    if not (isinstance(count, int) and count <= 0):
        eng.wait_ge(sem, count)


def graph_layers_kernel(nc, xt, adj, x, adjt, wk, wvt, awbv, ab, bk, w1, out):
    NP = xt.shape[0]
    LEAD, LAG = 3, 4
    WARM_UP = 12
    LOOP0 = 6
    LOOP1 = NP - LEAD - (NP - LEAD) % 2

    def there(r):
        return not isinstance(r, int) or 0 <= r < NP

    def steps(eng, step):
        for p in range(-LEAD, LOOP0):
            step(p, p % 2)
        with eng.Fori(LOOP0, LOOP1, 2) as i:
            step(i, 0)
            step(i + 1, 1)
        for p in range(LOOP1, NP + LAG):
            step(p, p % 2)

    def dma_count(r, k):
        return (r - k) * 8 + 16

    with ExitStack() as ctx:
        def sb(name, shape, dt=F32):
            return ctx.enter_context(nc.sbuf_tensor(name, shape, dt))

        def psum(name, shape):
            return ctx.enter_context(nc.psum_tensor(name, shape, F32))

        def sem(name):
            return ctx.enter_context(nc.semaphore(name))

        def sem2(name):
            return [sem(f"{name}_0"), sem(f"{name}_1")]

        ps_m = psum("ps_m", [P, GP, 512])
        ps_z = psum("ps_z", [P, GP, 512])
        ps_q = psum("ps_q", [P, GP, 512])
        ps_x = psum("ps_x", [P, GP, C, P])
        ps_u = psum("ps_u", [P, 2, GP, P])

        ident = sb("ident", [P, P])
        ones = sb("ones", [P, P])
        half = sb("half", [P, GP])
        wk_raw = sb("wk_raw", [P, C, 3 * D])
        w1_raw = sb("w1_raw", [P, C, 2 * D])
        w01_hi = sb("w01_hi", [P, C, 2 * D], F32R)
        w01_lo = sb("w01_lo", [P, C, 2 * D], F32R)
        w2s_hi = sb("w2s_hi", [P, C, D + 2], F32R)
        w2s_lo = sb("w2s_lo", [P, C, D + 2], F32R)
        w1_hi = sb("w1_hi", [P, C, 2 * D], F32R)
        w1_lo = sb("w1_lo", [P, C, 2 * D], F32R)
        wvt_sb = sb("wvt_sb", [P, C, D])
        awbv_sb = sb("awbv_sb", [P, C, 3])
        ws = sb("ws", [P, C, 2])
        cprod = sb("cprod", [P, 4])
        chalf = sb("chalf", [P, 1])
        bk_raw = sb("bk_raw", [P, D])
        bias = sb("bias", [P, D])
        table_out = sb("table_out", [P, 1])

        xt_raw = sb("xt_raw", [P, 2, GP * C * P])
        adj_sb = sb("adj_sb", [P, 2, GP * P])
        x_sb = sb("x_sb", [P, 2, GP * D])
        adjt_raw = sb("adjt_raw", [P, 2, GP * P])

        xt_hi = sb("xt_hi", [P, 2, GP * C * P], F32R)
        xt_lo = sb("xt_lo", [P, 2, GP * C * P], F32R)
        xw2_hi = sb("xw2_hi", [P, 2, GP, D], F32R)
        xw2_lo = sb("xw2_lo", [P, 2, GP, D], F32R)
        score = sb("score", [P, GP, 2])
        e_sum = sb("e_sum", [P, GP, P])
        e_leaky = sb("e_leaky", [P, GP * P])
        e_exp = sb("e_exp", [P, GP, P])
        alpha = sb("alpha", [P, GP, P])
        rowsum = sb("rowsum", [P, GP])
        rowinv = sb("rowinv", [P, GP])
        trans = sb("trans", [P, GP, P])
        tt_hi = sb("tt_hi", [P, GP, P], F32R)
        tt_lo = sb("tt_lo", [P, GP, P], F32R)
        z_hi = sb("z_hi", [P, GP, D], F32R)
        z_lo = sb("z_lo", [P, GP, D], F32R)
        hb = sb("hb", [P, GP, D])
        y1 = sb("y1", [P, GP, D])
        bn6 = sb("bn6", [P, GP, 6])
        mv = sb("mv", [P, GP, 2])
        var1 = sb("var1", [P, GP])
        rstd1 = sb("rstd1", [P, GP])
        x1 = sb("x1", [P, 2, GP, D])
        x1t_hi = sb("x1t_hi", [P, GP, C, P], F32R)
        x1t_lo = sb("x1t_lo", [P, GP, C, P], F32R)
        adjt_hi = sb("adjt_hi", [P, 2, GP * P], F32R)
        adjt_lo = sb("adjt_lo", [P, 2, GP * P], F32R)
        self_sb = sb("self_sb", [P, GP, D])
        q_hi = sb("q_hi", [P, GP, D + 2], F32R)
        q_lo = sb("q_lo", [P, GP, D], F32R)
        deg = sb("deg", [P, GP])
        deginv = sb("deginv", [P, GP])
        o_sum = sb("o_sum", [P, GP, D])
        y2 = sb("y2", [P, 2, GP, D])
        sum2 = sb("sum2", [P, 2, GP])
        nmean2 = sb("nmean2", [P, 2, GP])
        sq_out = sb("sq_out", [P, GP, D])
        sq2 = sb("sq2", [P, 2, GP])
        var2 = sb("var2", [P, 2, GP])
        rstd2 = sb("rstd2", [P, 2, GP])
        shift2 = sb("shift2", [P, 2, GP])
        out_sb = sb("out_sb", [P, 2, GP, D])

        s_sw = sem("score_weights_loaded")
        s_w2_in, s_w01_in, s_w1_in = sem("w2_loaded"), sem("w01_loaded"), sem("w1_loaded")
        s_zero = sem("bias_rows_zeroed")
        s_bk = sem("bias_rows_loaded")
        s_fill = sem("ident_filled")
        s_id = sem("ident_ready")
        s_const = sem("consts_ready")
        s_ws = sem("score_weights_in_psum")
        s_ab = sem("ab_loaded")
        s_bsum, s_bias = sem("bias_sum_in_psum"), sem("bias_ready")
        s_cp = sem("score_const_products")
        s_cs = sem("score_const_in_psum")
        s_dset = sem("dve_setup_chain")
        s_w2s = sem("w2_and_score_weights_split")
        s_w01 = sem("w01_split")
        s_w1 = sem("w1_split")
        s_w01_hi, s_w1_hi = sem("w01_hi_ready"), sem("w1_hi_ready")
        s_chalf = sem("score_const_ready")
        xt_in, adj_in, x_in, adjt_in = sem2("xt_in"), sem2("adj_in"), sem2("x_in"), sem2("adjt_in")
        stored = sem2("out_stored")
        s_xt_hi, s_xt_lo, s_xt_used = sem("xt_hi_ready"), sem2("xt_lo_ready"), sem("xt_used")
        s_xw2 = sem2("xw2_in_psum")
        s_xw2_hi, s_xw2_lo = sem2("xw2_hi_ready"), sem2("xw2_lo_ready")
        s_score = sem("score_ready")
        s_u = sem("src_score_in_psum")
        s_esum, s_leaky, s_exp = sem("e_sum_ready"), sem("e_leaky_ready"), sem("e_exp_ready")
        s_alpha, s_rowinv, s_trans = sem("alpha_ready"), sem("rowinv_ready"), sem("trans_ready")
        s_tt, s_tt_hi, s_tt_lo = sem("tt_in_psum"), sem("tt_hi_ready"), sem("tt_lo_ready")
        s_z, s_z_hi, s_z_lo = sem2("z_in_psum"), sem2("z_hi_ready"), sem2("z_lo_ready")
        s_h = sem2("h_in_psum")
        s_hb, s_y1 = sem("hb_ready"), sem2("y1_ready")
        s_bn, s_mv, s_var1 = sem2("y1_stats"), sem2("mv_ready"), sem("var1_ready")
        s_rstd1 = sem("rstd1_ready")
        s_x1 = sem2("x1_ready")
        s_x1t, s_x1t_hi, s_x1t_lo = sem("x1t_in_psum"), sem2("x1t_hi_ready"), sem("x1t_lo_ready")
        s_adjt_hi, s_adjt_lo = sem("adjt_hi_ready"), sem("adjt_lo_ready")
        s_pq, s_q_hi, s_q_lo, s_self = sem2("x1w_in_psum"), sem2("q_hi_ready"), sem2("q_lo_ready"), sem2("self_ready")
        s_agg = sem2("agg_in_psum")
        s_deg, s_deginv = sem("deg_ready"), sem("deginv_ready")
        s_o = sem2("o_sum_ready")
        s_y2, s_nmean2, s_sq2, s_var2 = sem2("y2_ready"), sem("nmean2_ready"), sem2("sq2_ready"), sem("var2_ready")
        s_rstd2, s_shift2, s_out = sem("rstd2_ready"), sem("shift2_ready"), sem("out_ready")

        block = ctx.enter_context(nc.Block())

        @block.sync
        def _(sp):
            sp.dma_start(wk_raw[:, :, 2 * D:3 * D], wk[:, :, 2 * D:3 * D]).then_inc(s_w2_in, 16)

            def load_xt(r, k):
                wait_count(sp, s_xt_hi, r - 1)
                wait_count(sp, s_xt_lo[1], r - 1)
                sp.dma_start(xt_raw[:, k, :], xt[r]).then_inc(xt_in[k], 16)

            def load_adj(r, k):
                wait_count(sp, s_alpha, r - 1)
                sp.dma_start(adj_sb[:, k, :], adj[r]).then_inc(adj_in[k], 16)

            def load_x(r, k):
                wait_count(sp, s_y1[1], r - 1)
                sp.dma_start(x_sb[:, k, :], x[r]).then_inc(x_in[k], 16)

            def load_adjt(r, k):
                wait_count(sp, s_adjt_hi, r - 1)
                wait_count(sp, s_adjt_lo, r - 1)
                sp.dma_start(adjt_raw[:, k, :], adjt[r]).then_inc(adjt_in[k], 16)

            def store(r, k):
                sp.wait_ge(s_out, r + 1)
                sp.dma_start(out[r], out_sb[:, k, :, :].rearrange("p g d -> p (g d)")).then_inc(stored[k], 16)

            def step(p, k):
                if there(p - 4):
                    store(p - 4, k)
                if isinstance(p, int) and p == -1:
                    sp.dma_start(w1_raw[:], w1).then_inc(s_w1_in, 16)
                if there(p + 3):
                    load_xt(p + 3, 1 - k)
                if there(p + 2):
                    load_adj(p + 2, k)
                if there(p):
                    load_adjt(p, k)
                if there(p + 1):
                    load_x(p + 1, 1 - k)

            steps(sp, step)
            for k in range(2):
                sp.wait_ge(stored[k], 16 * ((NP + 1 - k) // 2))

        @block.tensor
        def _(pe):
            pe.wait_ge(s_const, 1)
            for _ in range(WARM_UP):
                nc.tensor.matmul(ps_u[:, 0, 0, :], ones[:, :], ones[:, :], start=True, stop=True)
            pe.wait_ge(s_sw, 32)
            for c in range(C):
                for k in range(C):
                    mm = nc.tensor.matmul(ps_m[:, 0, 2 * c:2 * c + 2], wvt_sb[:, k, c * P:(c + 1) * P],
                                          awbv_sb[:, k, 0:2], start=(k == 0), stop=(k == C - 1))
            mm.then_inc(s_ws, 1)
            pe.wait_ge(s_ab, 16)
            pe.wait_ge(s_cp, 1)
            nc.tensor.matmul(ps_z[:, 1, 0:3], ones[:, :], cprod[:, 0:3], start=True, stop=True).then_inc(s_cs, 1)
            pe.wait_ge(s_w2s, 1)
            pe.wait_ge(s_id, 1)

            def halves(acc, st_hi, st_lo, mv_hi, mv_lo, start, stop, wide=None):
                nc.tensor.matmul(acc(mv_hi), st_hi, mv_hi, start=start, stop=False, skip_group_check=True)
                nc.tensor.matmul(acc(mv_lo), st_hi, mv_lo, start=False, stop=False, skip_group_check=True)
                return nc.tensor.matmul(acc(mv_hi), st_lo, mv_hi, start=False, stop=stop, skip_group_check=True)

            def project2(r, k):
                pe.wait_ge(s_xt_hi, r + 1)
                for g in range(GP):
                    pe.wait_ge(s_xt_lo[g], r + 1)
                    wait_count(pe, s_xw2_lo[g], r)
                    for c in range(C):
                        cols = slice((g * C + c) * P, (g * C + c + 1) * P)
                        mm = halves(lambda m: ps_m[:, g, 0:m.shape[-1]], xt_hi[:, k, cols], xt_lo[:, k, cols],
                                    w2s_hi[:, c, :], w2s_lo[:, c, :], c == 0, c == C - 1)
                    mm.then_inc(s_xw2[g], 1)

            def project01(r, k, g):
                wait_count(pe, s_hb, r)
                for c in range(C):
                    cols = slice((g * C + c) * P, (g * C + c + 1) * P)
                    mm = halves(lambda m: ps_z[:, g, 0:m.shape[-1]], xt_hi[:, k, cols], xt_lo[:, k, cols],
                                w01_hi[:, c, :], w01_lo[:, c, :], c == 0, False)
                if g == GP - 1:
                    mm.then_inc(s_xt_used, 1)

            def spread_source(r):
                pe.wait_ge(s_score, r + 1)
                wait_count(pe, s_tt_lo, r)
                for g in range(GP):
                    mm = nc.tensor.transpose(ps_u[:, 0, g, :], score[:, g, 0:1].to_broadcast([P, P]), ident[:, :])
                mm.then_inc(s_u, 1)

            def transpose_t(r):
                pe.wait_ge(s_trans, r + 1)
                for g in range(GP):
                    mm = nc.tensor.transpose(ps_u[:, 1, g, :], trans[:, g, :], ident[:, :])
                mm.then_inc(s_tt, 1)

            def hop1(r, k):
                pe.wait_ge(s_tt_hi, r + 1)
                pe.wait_ge(s_tt_lo, r + 1)
                for g in range(GP):
                    pe.wait_ge(s_xw2_hi[g], r + 1)
                    pe.wait_ge(s_xw2_lo[g], r + 1)
                    halves(lambda m: ps_z[:, g, D:2 * D], tt_hi[:, g, :], tt_lo[:, g, :],
                           xw2_hi[:, k, g, :], xw2_lo[:, k, g, :], False, False).then_inc(s_z[g], 1)

            def hop2(r):
                for g in range(GP):
                    pe.wait_ge(s_z_hi[g], r + 1)
                    pe.wait_ge(s_z_lo[g], r + 1)
                    halves(lambda m: ps_z[:, g, 0:D], tt_hi[:, g, :], tt_lo[:, g, :],
                           z_hi[:, g, :], z_lo[:, g, :], False, True).then_inc(s_h[g], 1)

            def transpose_x1(r, k):
                wait_count(pe, s_x1t_lo, r)
                for g in range(GP):
                    pe.wait_ge(s_x1[g], r + 1)
                    for c in range(C):
                        mm = nc.tensor.transpose(ps_x[:, g, c, :], x1[:, k, g, c * P:(c + 1) * P], ident[:, :])
                mm.then_inc(s_x1t, 1)

            def project_x1(r, g):
                pe.wait_ge(s_x1t_hi[g], r + 1)
                wait_count(pe, s_o[g], r)
                for c in range(C):
                    nc.tensor.matmul(ps_q[:, g, :], x1t_hi[:, g, c, :], w1_hi[:, c, :], start=(c == 0),
                                     stop=False, skip_group_check=True)
                    nc.tensor.matmul(ps_q[:, g, :], x1t_hi[:, g, c, :], w1_lo[:, c, :], start=False,
                                     stop=False, skip_group_check=True)
                pe.wait_ge(s_x1t_lo, r + 1)
                for c in range(C):
                    mm = nc.tensor.matmul(ps_q[:, g, :], x1t_lo[:, g, c, :], w1_hi[:, c, :], start=False,
                                          stop=(c == C - 1), skip_group_check=True)
                mm.then_inc(s_pq[g], 1)

            def aggregate(r, k):
                pe.wait_ge(s_adjt_hi, r + 1)
                pe.wait_ge(s_adjt_lo, r + 1)
                for g in range(GP):
                    pe.wait_ge(s_self[g], r + 1)
                    pe.wait_ge(s_q_hi[g], r + 1)
                    pe.wait_ge(s_q_lo[g], r + 1)
                    cols = slice(g * P, (g + 1) * P)
                    halves(lambda m: ps_q[:, g, 0:m.shape[-1]], adjt_hi[:, k, cols], adjt_lo[:, k, cols],
                           q_hi[:, g, :], q_lo[:, g, :], True, True).then_inc(s_agg[g], 1)

            def step(p, k):
                if there(p + 1):
                    project2(p + 1, 1 - k)
                first = isinstance(p, int) and p == 0
                if isinstance(p, int) and p == -1:
                    pe.wait_ge(s_bk, 16)
                    nc.tensor.matmul(ps_q[:, 0, 0:D], ones[:, :], bk_raw[:, :], start=True,
                                     stop=True).then_inc(s_bsum, 1)
                    spread_source(0)
                    pe.wait_ge(s_w01, 1)
                    project01(0, 0, 0)
                if first:
                    project01(0, 0, 1)
                elif there(p):
                    project01(p, k, 0)
                if there(p - 2):
                    aggregate(p - 2, k)
                if there(p):
                    transpose_t(p)
                    if not first:
                        project01(p, k, 1)
                if there(p - 1):
                    transpose_x1(p - 1, 1 - k)
                if there(p):
                    hop1(p, k)
                if there(p + 1) and not (isinstance(p, int) and p == -1):
                    spread_source(p + 1)
                if isinstance(p, int) and p == 1:
                    pe.wait_ge(s_w1, 1)
                    pe.wait_ge(s_bias, 1)
                if there(p - 1):
                    project_x1(p - 1, 0)
                if there(p):
                    hop2(p)
                if there(p - 1):
                    project_x1(p - 1, 1)

            steps(pe, step)

        @block.scalar
        def _(act):
            def copy_score(r):
                act.wait_ge(s_xw2[0], r + 1)
                act.wait_ge(s_xw2[1], r + 1)
                wait_count(act, s_u, r)
                nc.scalar.activation(score[:, :, :], ps_m[:, :, D:D + 2], ACT.Identity,
                                     bias=chalf[:, 0:1]).then_inc(s_score, 1)

            def split_xw2(r, k, g):
                wait_count(act, s_z[g], r - 1)
                nc.scalar.activation(xw2_hi[:, k, g, :], ps_m[:, g, 0:D], ACT.Copy).then_inc(s_xw2_hi[g], 1)

            def split_tt(r):
                act.wait_ge(s_tt, r + 1)
                wait_count(act, s_h[1], r)
                nc.scalar.activation(tt_hi[:, :, :], ps_u[:, 1, :, :], ACT.Copy).then_inc(s_tt_hi, 1)

            def split_adjt(r, k):
                act.wait_ge(adjt_in[k], dma_count(r, k))
                wait_count(act, s_agg[1], r - 1)
                nc.scalar.activation(adjt_hi[:, k, :], adjt_raw[:, k, :], ACT.Copy).then_inc(s_adjt_hi, 1)

            def split_x1t(r):
                act.wait_ge(s_x1t, r + 1)
                wait_count(act, s_pq[1], r)
                for g in range(GP):
                    nc.scalar.activation(x1t_hi[:, g, :, :], ps_x[:, g, :, :], ACT.Copy).then_inc(s_x1t_hi[g], 1)

            def add_scores(r):
                act.wait_ge(s_u, r + 1)
                act.wait_ge(s_score, r + 1)
                wait_count(act, s_leaky, r)
                for g in range(GP):
                    a = nc.scalar.activation(e_sum[:, g, :], ps_u[:, 0, g, :], ACT.Identity,
                                             bias=score[:, g, 1:2])
                a.then_inc(s_esum, 1)

            def split_z(r, g):
                act.wait_ge(s_z[g], r + 1)
                wait_count(act, s_h[g], r)
                nc.scalar.activation(z_hi[:, g, :], ps_z[:, g, D:2 * D], ACT.Copy).then_inc(s_z_hi[g], 1)

            def square_y2(r, k):
                act.wait_ge(s_nmean2, r + 1)
                wait_count(act, s_var2, r - 1)
                for g in range(GP):
                    wait_count(act, s_sq2[g], r)
                    nc.scalar.activation(sq_out[:, g, :], y2[:, k, g, :], ACT.Square, bias=nmean2[:, k, g:g + 1],
                                         accum_out=sq2[:, k, g:g + 1]).then_inc(s_sq2[g], 1)

            def split_xt(r, k):
                act.wait_ge(xt_in[k], dma_count(r, k))
                wait_count(act, s_xt_used, r - 1)
                nc.scalar.activation(xt_hi[:, k, :], xt_raw[:, k, :], ACT.Copy).then_inc(s_xt_hi, 1)

            def exponential(r):
                act.wait_ge(s_leaky, r + 1)
                wait_count(act, s_alpha, r)
                nc.scalar.activation(e_exp[:, :, :], e_leaky[:, :].rearrange("p (g n) -> p g n", g=GP),
                                     ACT.Exp).then_inc(s_exp, 1)

            def split_q(r, g):
                act.wait_ge(s_pq[g], r + 1)
                wait_count(act, s_o[g], r)
                nc.scalar.activation(self_sb[:, g, :], ps_q[:, g, 0:D], ACT.Copy).then_inc(s_self[g], 1)
                wait_count(act, s_agg[g], r)
                nc.scalar.activation(q_hi[:, g, 0:D], ps_q[:, g, D:2 * D], ACT.Copy).then_inc(s_q_hi[g], 1)

            def scale_rows(r):
                act.wait_ge(s_rowinv, r + 1)
                wait_count(act, s_tt, r)
                for g in range(GP):
                    a = nc.scalar.activation(trans[:, g, :], alpha[:, g, :], ACT.Copy, scale=rowinv[:, g:g + 1])
                a.then_inc(s_trans, 1)

            act.dma_start(wvt_sb[:], wvt).then_inc(s_sw, 16)
            act.dma_start(awbv_sb[:], awbv).then_inc(s_sw, 16)
            act.dma_start(wk_raw[:, :, 0:2 * D], wk[:, :, 0:2 * D]).then_inc(s_w01_in, 16)
            act.wait_ge(s_const, 1)
            nc.scalar.activation(table_out[:, :], ones[:, 0:1], ACT.Exp)

            def step(p, k):
                filling = isinstance(p, int) and p < 0
                if filling and there(p + 2):
                    split_xt(p + 2, k)
                if filling and p == -1:
                    act.wait_ge(s_w01_in, 16)
                    nc.scalar.activation(w01_hi[:, :, :], wk_raw[:, :, 0:2 * D], ACT.Copy).then_inc(s_w01_hi, 1)
                    act.wait_ge(s_chalf, 1)
                if there(p - 2):
                    split_q(p - 2, 1)
                if there(p + 1):
                    copy_score(p + 1)
                    split_xw2(p + 1, 1 - k, 0)
                    split_xw2(p + 1, 1 - k, 1)
                if filling and p == -1:
                    act.wait_ge(s_w1_in, 16)
                    nc.scalar.activation(w1_hi[:, :, :], w1_raw[:, :, :], ACT.Copy).then_inc(s_w1_hi, 1)
                if there(p):
                    split_tt(p)
                if isinstance(p, int) and p == 0:
                    split_xt(2, 0)
                if there(p - 1):
                    split_adjt(p - 1, 1 - k)
                if there(p - 3):
                    square_y2(p - 3, 1 - k)
                if there(p - 1):
                    split_x1t(p - 1)
                if there(p):
                    split_z(p, 0)
                    split_z(p, 1)
                if there(p + 1):
                    add_scores(p + 1)
                if not (isinstance(p, int) and p <= 0) and there(p + 2):
                    split_xt(p + 2, k)
                if there(p + 1):
                    exponential(p + 1)
                if there(p - 1):
                    split_q(p - 1, 0)
                if there(p + 1):
                    scale_rows(p + 1)

            steps(act, step)

        @block.gpsimd
        def _(pool):
            nc.gpsimd.memset(cprod[:], 0.0).then_inc(s_zero, 1)
            nc.gpsimd.memset(bk_raw[:], 0.0).then_inc(s_zero, 1)
            pool.wait_ge(s_zero, 2)
            pool.dma_start(cprod[0:1, 2:3], ab).then_inc(s_ab, 16)
            pool.dma_start(bk_raw[0:3, :], bk).then_inc(s_bk, 16)
            nc.gpsimd.memset(ident[:], 0.0).then_inc(s_fill, 1)
            nc.gpsimd.memset(half[:], -0.5).then_inc(s_fill, 1)
            pool.wait_ge(s_fill, 2)
            nc.gpsimd.affine_select(out=ident[:], in_=ident[:], compare_op=ALU.not_equal, fill=1.0, base=0,
                                    pattern=[[-1, P]], channel_multiplier=1).then_inc(s_id, 1)

            def rstd_of_y1(r):
                pool.wait_ge(s_var1, r + 1)
                wait_count(pool, s_x1[1], r)
                nc.gpsimd.tensor_tensor(rstd1[:, :], var1[:, :], half[:, :], ALU.pow).then_inc(s_rstd1, 1)

            def split_adjt(r, k):
                pool.wait_ge(s_adjt_hi, r + 1)
                wait_count(pool, s_agg[1], r - 1)
                nc.gpsimd.tensor_tensor(adjt_lo[:, k, :], adjt_raw[:, k, :], adjt_hi[:, k, :].bitcast(F32),
                                        ALU.subtract).then_inc(s_adjt_lo, 1)

            def y2_scale_ready(r, k):
                wait_count(pool, stored[k], dma_count(r - 2, k))
                pool.wait_ge(s_shift2, r + 1)

            def normalise_y2(r, k):
                for g in range(GP):
                    t = nc.gpsimd.tensor_scalar(out_sb[:, k, g, :], y2[:, k, g, :], rstd2[:, k, g:g + 1],
                                                shift2[:, k, g:g + 1], ALU.mult, ALU.add)
                t.then_inc(s_out, 1)

            def split_xt(r, k):
                pool.wait_ge(s_xt_hi, r + 1)
                wait_count(pool, s_xt_used, r - 1)
                for g in range(GP):
                    cols = slice(g * C * P, (g + 1) * C * P)
                    nc.gpsimd.tensor_tensor(xt_lo[:, k, cols], xt_raw[:, k, cols], xt_hi[:, k, cols].bitcast(F32),
                                            ALU.subtract).then_inc(s_xt_lo[g], 1)

            def rstd_of_y2(r, k):
                pool.wait_ge(s_var2, r + 1)
                nc.gpsimd.tensor_tensor(rstd2[:, k, :], var2[:, k, :], half[:, :], ALU.pow).then_inc(s_rstd2, 1)
                pool.wait_ge(s_rstd2, r + 1)
                nc.gpsimd.tensor_tensor(shift2[:, k, :], rstd2[:, k, :], nmean2[:, k, :],
                                        ALU.mult).then_inc(s_shift2, 1)

            def step(p, k):
                if there(p - 1):
                    rstd_of_y1(p - 1)
                    split_adjt(p - 1, 1 - k)
                if there(p - 3):
                    rstd_of_y2(p - 3, 1 - k)
                    y2_scale_ready(p - 3, 1 - k)
                if there(p + 2):
                    split_xt(p + 2, k)
                if isinstance(p, int) and p == -1:
                    pool.wait_ge(s_w1_hi, 1)
                    nc.gpsimd.tensor_tensor(w1_lo[:, :, :], w1_raw[:, :, :], w1_hi[:, :, :].bitcast(F32),
                                            ALU.subtract).then_inc(s_w1, 1)
                if there(p - 3):
                    normalise_y2(p - 3, 1 - k)

            steps(pool, step)

        @block.vector
        def _(dve):
            links = [0]

            def link(ins):
                links[0] += 1
                ins.then_inc(s_dset, 1)
                dve.wait_ge(s_dset, links[0])

            nc.vector.memset(ones[:], 1.0).then_inc(s_const, 1)
            dve.wait_ge(s_const, 1)
            for g in range(GP):
                link(nc.vector.tensor_copy(q_hi[:, g, D:D + 2], ones[:, 0:2]))
            dve.wait_ge(s_sw, 32)
            dve.wait_ge(s_zero, 2)
            link(nc.vector.tensor_tensor(cprod[:, 0:C], awbv_sb[:, :, 0], awbv_sb[:, :, 1], ALU.add))
            nc.vector.tensor_tensor(cprod[:, 0:C], cprod[:, 0:C], awbv_sb[:, :, 2], ALU.mult).then_inc(s_cp, 1)
            dve.wait_ge(s_w2_in, 16)
            w2 = wk_raw[:, :, 2 * D:3 * D]
            link(nc.vector.tensor_copy(w2s_hi[:, :, 0:D], w2))
            nc.vector.tensor_tensor(w2s_lo[:, :, 0:D], w2, w2s_hi[:, :, 0:D].bitcast(F32), ALU.subtract)
            dve.wait_ge(s_ws, 1)
            link(nc.vector.tensor_copy(ws[:, :, :], ps_m[:, 0, 0:2 * C].rearrange("p (c s) -> p c s", c=C)))
            link(nc.vector.tensor_copy(w2s_hi[:, :, D:D + 2], ws[:, :, :]))
            nc.vector.tensor_tensor(w2s_lo[:, :, D:D + 2], ws[:, :, :],
                                    w2s_hi[:, :, D:D + 2].bitcast(F32), ALU.subtract).then_inc(s_w2s, 1)
            dve.wait_ge(s_cs, 1)
            link(nc.vector.reduce_sum(chalf[:, :], ps_z[:, 1, 0:3], axis=mybir.AxisListType.X))
            nc.vector.tensor_scalar(chalf[:, :], chalf[:, :], 0.5, None, ALU.mult).then_inc(s_chalf, 1)
            dve.wait_ge(s_w01_hi, 1)
            nc.vector.tensor_tensor(w01_lo[:, :, :], wk_raw[:, :, 0:2 * D], w01_hi[:, :, :].bitcast(F32),
                                    ALU.subtract).then_inc(s_w01, 1)

            def add_bias(r):
                dve.wait_ge(s_h[0], r + 1)
                dve.wait_ge(s_h[1], r + 1)
                nc.vector.tensor_tensor(hb[:, :, :], ps_z[:, :, 0:D],
                                        bias[:, :].unsqueeze(1).to_broadcast([P, GP, D]), ALU.add).then_inc(s_hb, 1)

            def residual1(r, k):
                dve.wait_ge(x_in[k], dma_count(r, k))
                dve.wait_ge(s_hb, r + 1)
                wait_count(dve, s_x1[1], r)
                for g in range(GP):
                    nc.vector.scalar_tensor_tensor(out=y1[:, g, :], in0=hb[:, g, :], scalar=0.0,
                                                   in1=x_sb[:, k, g * D:(g + 1) * D], op0=ALU.max,
                                                   op1=ALU.add).then_inc(s_y1[g], 1)

            def statistics1(r):
                for g in range(GP):
                    dve.wait_ge(s_y1[g], r + 1)
                    nc.vector.bn_stats(bn6[:, g, :], y1[:, g, :]).then_inc(s_bn[g], 1)

            def stats1_written(r):
                dve.wait_ge(s_bn[0], r + 1)
                dve.wait_ge(s_bn[1], r + 1)

            def moments1(r):
                for g in range(GP):
                    nc.vector.bn_aggr(mv[:, g, :], bn6[:, g, :]).then_inc(s_mv[g], 1)
                dve.wait_ge(s_mv[0], r + 1)
                dve.wait_ge(s_mv[1], r + 1)
                wait_count(dve, s_rstd1, r)
                nc.vector.tensor_scalar(var1[:, :], mv[:, :, 1], LN_EPS, None, ALU.add).then_inc(s_var1, 1)

            def split_xw2(r, k, g):
                dve.wait_ge(s_score, r + 1)
                dve.wait_ge(s_xw2_hi[g], r + 1)
                wait_count(dve, s_z[g], r - 1)
                nc.vector.tensor_tensor(xw2_lo[:, k, g, :], ps_m[:, g, 0:D], xw2_hi[:, k, g, :].bitcast(F32),
                                        ALU.subtract).then_inc(s_xw2_lo[g], 1)

            def split_tt(r):
                dve.wait_ge(s_tt_hi, r + 1)
                wait_count(dve, s_h[1], r)
                nc.vector.tensor_tensor(tt_lo[:, :, :], ps_u[:, 1, :, :], tt_hi[:, :, :].bitcast(F32),
                                        ALU.subtract).then_inc(s_tt_lo, 1)

            def normalise_y1(r, k):
                dve.wait_ge(s_rstd1, r + 1)
                wait_count(dve, s_x1t, r - 1)
                for g in range(GP):
                    nc.vector.tensor_scalar(x1[:, k, g, :], y1[:, g, :], mv[:, g, 0:1], rstd1[:, g:g + 1],
                                            ALU.subtract, ALU.mult).then_inc(s_x1[g], 1)

            def degree(r):
                dve.wait_ge(s_agg[0], r + 1)
                dve.wait_ge(s_agg[1], r + 1)
                nc.vector.tensor_scalar(deg[:, :], ps_q[:, :, D], DEG_EPS, None, ALU.max).then_inc(s_deg, 1)

            def degree_inverse(r):
                dve.wait_ge(s_deg, r + 1)
                nc.vector.reciprocal(deginv[:, :], deg[:, :]).then_inc(s_deginv, 1)

            def add_aggregate(r):
                dve.wait_ge(s_deginv, r + 1)
                for g in range(GP):
                    dve.wait_ge(s_self[g], r + 1)
                    nc.vector.scalar_tensor_tensor(out=o_sum[:, g, :], in0=ps_q[:, g, 0:D],
                                                   scalar=deginv[:, g:g + 1], in1=self_sb[:, g, :],
                                                   op0=ALU.mult, op1=ALU.add).then_inc(s_o[g], 1)

            def residual2(r, k):
                wait_count(dve, s_out, r - 1)
                wait_count(dve, s_sq2[1], r - 1)
                for g in range(GP):
                    dve.wait_ge(s_o[g], r + 1)
                    nc.vector.scalar_tensor_tensor(out=y2[:, k, g, :], in0=o_sum[:, g, :], scalar=0.0,
                                                   in1=x1[:, k, g, :], op0=ALU.max, op1=ALU.add,
                                                   accum_out=sum2[:, k, g:g + 1]).then_inc(s_y2[g], 1)

            def mean2(r, k):
                dve.wait_ge(s_y2[0], r + 1)
                dve.wait_ge(s_y2[1], r + 1)
                wait_count(dve, s_shift2, r - 1)
                nc.vector.tensor_scalar(nmean2[:, k, :], sum2[:, k, :], -1.0 / D, None,
                                        ALU.mult).then_inc(s_nmean2, 1)

            def split_x1t(r):
                dve.wait_ge(s_x1t_hi[0], r + 1)
                dve.wait_ge(s_x1t_hi[1], r + 1)
                wait_count(dve, s_pq[1], r)
                nc.vector.tensor_tensor(x1t_lo[:, :, :, :], ps_x[:, :, :, :], x1t_hi[:, :, :, :].bitcast(F32),
                                        ALU.subtract).then_inc(s_x1t_lo, 1)

            def leaky(r):
                dve.wait_ge(s_esum, r + 1)
                wait_count(dve, s_exp, r)
                e = e_sum[:, :, :].rearrange("p g n -> p (g n)")
                nc.vector.scalar_tensor_tensor(out=e_leaky[:, :], in0=e, scalar=LEAK, in1=e, op0=ALU.mult,
                                               op1=ALU.max).then_inc(s_leaky, 1)

            def split_z(r, g):
                dve.wait_ge(s_z_hi[g], r + 1)
                wait_count(dve, s_h[g], r)
                nc.vector.tensor_tensor(z_lo[:, g, :], ps_z[:, g, D:2 * D], z_hi[:, g, :].bitcast(F32),
                                        ALU.subtract).then_inc(s_z_lo[g], 1)

            def weigh(r, k):
                dve.wait_ge(adj_in[k], dma_count(r, k))
                dve.wait_ge(s_exp, r + 1)
                wait_count(dve, s_trans, r)
                for g in range(GP):
                    a = nc.vector.tensor_tensor_reduce(alpha[:, g, :], adj_sb[:, k, g * P:(g + 1) * P],
                                                       e_exp[:, g, :], 1.0, ROW_EPS, ALU.mult, ALU.add,
                                                       rowsum[:, g:g + 1])
                a.then_inc(s_alpha, 1)
                dve.wait_ge(s_alpha, r + 1)
                nc.vector.reciprocal(rowinv[:, :], rowsum[:, :]).then_inc(s_rowinv, 1)

            def variance2(r, k):
                dve.wait_ge(s_sq2[0], r + 1)
                dve.wait_ge(s_sq2[1], r + 1)
                wait_count(dve, s_rstd2, r - 1)
                nc.vector.tensor_scalar(var2[:, k, :], sq2[:, k, :], 1.0 / D, LN_EPS, ALU.mult,
                                        ALU.add).then_inc(s_var2, 1)

            def split_q(r, g):
                dve.wait_ge(s_q_hi[g], r + 1)
                wait_count(dve, s_agg[g], r)
                nc.vector.tensor_tensor(q_lo[:, g, :], ps_q[:, g, D:2 * D], q_hi[:, g, 0:D].bitcast(F32),
                                        ALU.subtract).then_inc(s_q_lo[g], 1)

            def step(p, k):
                if there(p - 1):
                    statistics1(p - 1)
                    stats1_written(p - 1)
                if there(p - 2):
                    split_q(p - 2, 1)
                if there(p - 1):
                    moments1(p - 1)
                if there(p + 1):
                    split_xw2(p + 1, 1 - k, 0)
                    split_xw2(p + 1, 1 - k, 1)
                if there(p - 1):
                    normalise_y1(p - 1, 1 - k)
                if there(p - 2):
                    degree(p - 2)
                if there(p):
                    split_tt(p)
                if there(p - 2):
                    degree_inverse(p - 2)
                if there(p - 2):
                    add_aggregate(p - 2)
                if there(p - 1):
                    split_x1t(p - 1)
                if there(p - 3):
                    variance2(p - 3, 1 - k)
                if there(p):
                    split_z(p, 0)
                    split_z(p, 1)
                if there(p + 1):
                    leaky(p + 1)
                if there(p - 2):
                    residual2(p - 2, k)
                if isinstance(p, int) and p == -1:
                    dve.wait_ge(s_bsum, 1)
                    nc.vector.tensor_copy(bias[:, :], ps_q[:, 0, 0:D]).then_inc(s_bias, 1)
                if there(p):
                    if isinstance(p, int) and p == 0:
                        dve.wait_ge(s_bias, 1)
                    add_bias(p)
                if there(p - 2):
                    mean2(p - 2, k)
                if there(p + 1):
                    weigh(p + 1, 1 - k)
                if there(p):
                    residual1(p, k)
                if there(p - 1):
                    split_q(p - 1, 0)

            steps(dve, step)


def kernel(x, adj, L0_gnn_Wv, L0_gnn_bv, L0_gnn_aw, L0_gnn_ab, L0_gnn_Wk, L0_gnn_bk, L1_gnn_W):
    import numpy as np
    import concourse.bacc as bacc
    from concourse.bass_utils import run_bass_kernel_spmd

    x, adj = np.asarray(x), np.asarray(adj)
    Wv, bv, aw, ab = (np.asarray(a) for a in (L0_gnn_Wv, L0_gnn_bv, L0_gnn_aw, L0_gnn_ab))
    Wk, bk, W1 = np.asarray(L0_gnn_Wk), np.asarray(L0_gnn_bk), np.asarray(L1_gnn_W)
    B = x.shape[0]
    NP = B // GP

    def rows(a):
        return a.reshape(C, P, -1).transpose(1, 0, 2)

    arrays = {
        "in_xt": x.reshape(NP, GP, P, C, P).transpose(0, 4, 1, 3, 2).reshape(NP, P, GP * C * P),
        "in_adj": adj.reshape(NP, GP, P, P).transpose(0, 2, 1, 3).reshape(NP, P, GP * P),
        "in_x": x.reshape(NP, GP, P, D).transpose(0, 2, 1, 3).reshape(NP, P, GP * D),
        "in_adjt": adj.reshape(NP, GP, P, P).transpose(0, 3, 1, 2).reshape(NP, P, GP * P),
        "in_wk": rows(Wk.transpose(1, 0, 2).reshape(D, 3 * D)),
        "in_wvt": rows(Wv.T),
        "in_awbv": rows(np.concatenate([aw.reshape(2, D), bv.reshape(1, D)]).T),
        "in_ab": ab.reshape(1, 1),
        "in_bk": bk,
        "in_w1": rows(W1.reshape(D, 2, D).transpose(2, 1, 0).reshape(D, 2 * D)),
    }
    arrays = {n: np.ascontiguousarray(a) for n, a in arrays.items()}
    nc = bacc.Bacc("TRN2", target_bir_lowering=False, num_devices=1)
    args = [nc.dram_tensor(n, a.shape, mybir.dt.from_np(a.dtype), kind="ExternalInput").ap()
            for n, a in arrays.items()]
    args.append(nc.dram_tensor("out_y", (NP, P, GP * D), F32, kind="ExternalOutput").ap())
    graph_layers_kernel(nc, *args)
    got = run_bass_kernel_spmd(nc, [arrays], core_ids=[0]).results[0]["out_y"]
    return got.reshape(NP, P, GP, D).transpose(0, 2, 1, 3).reshape(B, P, D)
```

```python
from contextlib import ExitStack

import concourse.bass as bass
from concourse import mybir

ALU = mybir.AluOpType
ACT = mybir.ActivationFunctionType
F32 = mybir.dt.float32
F32R = mybir.dt.float32r

P = 128
D = 256
C = D // P
GP = 2
LEAK = 0.2
LN_EPS = 1e-5
ROW_EPS = 1e-12
DEG_EPS = 1e-6


def wait_count(eng, sem, count):
    if not (isinstance(count, int) and count <= 0):
        eng.wait_ge(sem, count)


def graph_layers_kernel(nc, xt, adj, x, adjt, wk, wvt, awbv, ab, bk, w1, out):
    NP = xt.shape[0]
    LEAD, LAG = 3, 4
    WARM_UP, KEEP_UP = 12, 8
    LOOP0 = 6
    LOOP1 = NP - LEAD - (NP - LEAD) % 2

    def there(r):
        return not isinstance(r, int) or 0 <= r < NP

    def at(p, n):
        return isinstance(p, int) and p == n

    def steps(eng, step, last):
        for p in range(-LEAD, LOOP0):
            step(p, p % 2)
        with eng.Fori(LOOP0, LOOP1, 2) as i:
            step(i, 0)
            step(i + 1, 1)
        for p in range(LOOP1, NP + LAG):
            (last if p in (NP - 1, NP) else step)(p, p % 2)

    def dma_count(r, k):
        return (r - k) * 8 + 16

    with ExitStack() as ctx:
        def sb(name, shape, dt=F32):
            return ctx.enter_context(nc.sbuf_tensor(name, shape, dt))

        def psum(name, shape):
            return ctx.enter_context(nc.psum_tensor(name, shape, F32))

        def sem(name):
            return ctx.enter_context(nc.semaphore(name))

        def sem2(name):
            return [sem(f"{name}_0"), sem(f"{name}_1")]

        ps_m = psum("ps_m", [P, GP, 512])
        ps_z = psum("ps_z", [P, GP, 512])
        ps_q = psum("ps_q", [P, GP, 512])
        ps_x = psum("ps_x", [P, GP, C, P])
        ps_u = psum("ps_u", [P, 2, GP, P])

        def bank2(r):
            return ps_m if at(r, NP - 2) else ps_q

        ident = sb("ident", [P, P])
        ones = sb("ones", [P, P])
        half = sb("half", [P, GP])
        wk_raw = sb("wk_raw", [P, C, 3 * D])
        w1_raw = sb("w1_raw", [P, C, 2 * D])
        w01_hi = sb("w01_hi", [P, C, 2 * D], F32R)
        w01_lo = sb("w01_lo", [P, C, 2 * D], F32R)
        w2s_hi = sb("w2s_hi", [P, C, D + 2], F32R)
        w2s_lo = sb("w2s_lo", [P, C, D + 2], F32R)
        w1_hi = sb("w1_hi", [P, C, 2 * D], F32R)
        w1_lo = sb("w1_lo", [P, C, 2 * D], F32R)
        wvt_sb = sb("wvt_sb", [P, C, D])
        awbv_sb = sb("awbv_sb", [P, C, 3])
        cprod = sb("cprod", [P, 4])
        chalf = sb("chalf", [P, 1])
        bk_raw = sb("bk_raw", [P, D])
        bias = sb("bias", [P, D])
        table_out = sb("table_out", [P, 1])

        xt_raw = sb("xt_raw", [P, 2, GP * C * P])
        adj_sb = sb("adj_sb", [P, 2, GP * P])
        x_sb = sb("x_sb", [P, 2, GP * D])
        adjt_raw = sb("adjt_raw", [P, 2, GP * P])

        xt_hi = sb("xt_hi", [P, 2, GP * C * P], F32R)
        xt_lo = sb("xt_lo", [P, 2, GP * C * P], F32R)
        xw2_hi = sb("xw2_hi", [P, 2, GP, D], F32R)
        xw2_lo = sb("xw2_lo", [P, 2, GP, D], F32R)
        score = sb("score", [P, GP, 2])
        e_sum = sb("e_sum", [P, GP, P])
        e_leaky = sb("e_leaky", [P, GP * P])
        e_exp = sb("e_exp", [P, GP, P])
        alpha = sb("alpha", [P, GP, P])
        rowsum = sb("rowsum", [P, GP])
        rowinv = sb("rowinv", [P, GP])
        trans = sb("trans", [P, GP, P])
        tt_hi = sb("tt_hi", [P, GP, P], F32R)
        tt_lo = sb("tt_lo", [P, GP, P], F32R)
        z_hi = sb("z_hi", [P, GP, D], F32R)
        z_lo = sb("z_lo", [P, GP, D], F32R)
        hb = sb("hb", [P, GP, D])
        y1 = sb("y1", [P, GP, D])
        bn6 = sb("bn6", [P, GP, 6])
        mv = sb("mv", [P, GP, 2])
        var1 = sb("var1", [P, GP])
        rstd1 = sb("rstd1", [P, GP])
        x1 = sb("x1", [P, 2, GP, D])
        x1t_hi = sb("x1t_hi", [P, GP, C, P], F32R)
        x1t_lo = sb("x1t_lo", [P, GP, C, P], F32R)
        adjt_hi = sb("adjt_hi", [P, 2, GP * P], F32R)
        adjt_lo = sb("adjt_lo", [P, 2, GP * P], F32R)
        self_sb = sb("self_sb", [P, GP, D])
        q_hi = sb("q_hi", [P, GP, D + 2], F32R)
        q_lo = sb("q_lo", [P, GP, D], F32R)
        deg = sb("deg", [P, GP])
        deginv = sb("deginv", [P, GP])
        o_sum = sb("o_sum", [P, GP, D])
        y2 = sb("y2", [P, 2, GP, D])
        sum2 = sb("sum2", [P, 2, GP])
        nmean2 = sb("nmean2", [P, 2, GP])
        sq_out = sb("sq_out", [P, GP, D])
        sq2 = sb("sq2", [P, 2, GP])
        var2 = sb("var2", [P, 2, GP])
        rstd2 = sb("rstd2", [P, 2, GP])
        shift2 = sb("shift2", [P, 2, GP])
        out_sb = sb("out_sb", [P, 2, GP, D])

        s_sw = sem("score_weights_loaded")
        s_w2_in, s_w01_in, s_w1_in = sem("w2_loaded"), sem("w01_loaded"), sem("w1_loaded")
        s_zero = sem("bias_rows_zeroed")
        s_bk = sem("bias_rows_loaded")
        s_fill = sem("ident_filled")
        s_id = sem("ident_ready")
        s_const = sem("consts_ready")
        s_ws = sem("score_weights_in_psum")
        s_ab = sem("ab_loaded")
        s_bsum, s_bias = sem("bias_sum_in_psum"), sem("bias_ready")
        s_cp = sem("score_const_products")
        s_cs = sem("score_const_in_psum")
        s_dset = sem("dve_setup_chain")
        s_w2s = sem("w2_and_score_weights_split")
        s_w01 = sem("w01_split")
        s_w1 = sem("w1_split")
        s_w01_hi, s_w1_hi = sem("w01_hi_ready"), sem("w1_hi_ready")
        s_chalf = sem("score_const_ready")
        xt_in, adj_in, x_in, adjt_in = sem2("xt_in"), sem2("adj_in"), sem2("x_in"), sem2("adjt_in")
        stored = sem2("out_stored")
        s_xt_hi, s_xt_lo, s_xt_used = sem("xt_hi_ready"), sem2("xt_lo_ready"), sem("xt_used")
        s_xw2 = sem2("xw2_in_psum")
        s_xw2_hi, s_xw2_lo = sem2("xw2_hi_ready"), sem2("xw2_lo_ready")
        s_score = sem("score_ready")
        s_u = sem("src_score_in_psum")
        s_esum, s_leaky, s_exp = sem("e_sum_ready"), sem("e_leaky_ready"), sem("e_exp_ready")
        s_alpha, s_rowinv, s_trans = sem("alpha_ready"), sem("rowinv_ready"), sem("trans_ready")
        s_tt, s_tt_hi, s_tt_lo = sem("tt_in_psum"), sem("tt_hi_ready"), sem("tt_lo_ready")
        s_z, s_z_hi, s_z_lo = sem2("z_in_psum"), sem2("z_hi_ready"), sem2("z_lo_ready")
        s_h = sem2("h_in_psum")
        s_hb, s_y1 = sem("hb_ready"), sem2("y1_ready")
        s_bn, s_mv, s_var1 = sem2("y1_stats"), sem2("mv_ready"), sem("var1_ready")
        s_rstd1 = sem("rstd1_ready")
        s_x1 = sem2("x1_ready")
        s_x1t, s_x1t_hi, s_x1t_lo = sem("x1t_in_psum"), sem2("x1t_hi_ready"), sem("x1t_lo_ready")
        s_adjt_hi, s_adjt_lo = sem("adjt_hi_ready"), sem("adjt_lo_ready")
        s_pq, s_q_hi, s_q_lo, s_self = sem2("x1w_in_psum"), sem2("q_hi_ready"), sem2("q_lo_ready"), sem2("self_ready")
        s_agg = sem2("agg_in_psum")
        s_deg, s_deginv = sem("deg_ready"), sem("deginv_ready")
        s_o = sem2("o_sum_ready")
        s_y2, s_nmean2, s_sq2, s_var2 = sem2("y2_ready"), sem("nmean2_ready"), sem2("sq2_ready"), sem("var2_ready")
        s_rstd2, s_shift2, s_out = sem("rstd2_ready"), sem("shift2_ready"), sem("out_ready")
        s_out_last = sem("last_out_ready")

        block = ctx.enter_context(nc.Block())

        @block.sync
        def _(sp):
            sp.dma_start(wk_raw[:, :, 2 * D:3 * D], wk[:, :, 2 * D:3 * D]).then_inc(s_w2_in, 16)

            def load_xt(r, k):
                wait_count(sp, s_xt_hi, r - 1)
                wait_count(sp, s_xt_lo[1], r - 1)
                sp.dma_start(xt_raw[:, k, :], xt[r]).then_inc(xt_in[k], 16)

            def load_adj(r, k):
                wait_count(sp, s_alpha, r - 1)
                sp.dma_start(adj_sb[:, k, :], adj[r]).then_inc(adj_in[k], 16)

            def load_x(r, k):
                wait_count(sp, s_y1[1], r - 1)
                sp.dma_start(x_sb[:, k, :], x[r]).then_inc(x_in[k], 16)

            def load_adjt(r, k):
                wait_count(sp, s_adjt_hi, r - 1)
                wait_count(sp, s_adjt_lo, r - 1)
                sp.dma_start(adjt_raw[:, k, :], adjt[r]).then_inc(adjt_in[k], 16)

            def store(r, k):
                if at(r, NP - 1):
                    sp.wait_ge(s_out_last, GP)
                else:
                    sp.wait_ge(s_out, r + 1)
                sp.dma_start(out[r], out_sb[:, k, :, :].rearrange("p g d -> p (g d)")).then_inc(stored[k], 16)

            def step(p, k):
                if there(p - 4):
                    store(p - 4, k)
                if at(p, -1):
                    sp.dma_start(w1_raw[:], w1).then_inc(s_w1_in, 16)
                if there(p + 3):
                    load_xt(p + 3, 1 - k)
                if there(p + 2):
                    load_adj(p + 2, k)
                if there(p):
                    load_adjt(p, k)
                if there(p + 1):
                    load_x(p + 1, 1 - k)

            steps(sp, step, step)
            for k in range(2):
                sp.wait_ge(stored[k], 16 * ((NP + 1 - k) // 2))

        @block.tensor
        def _(pe):
            pe.wait_ge(s_const, 1)
            for _ in range(WARM_UP):
                nc.tensor.matmul(ps_u[:, 0, 0, :], ones[:, :], ones[:, :], start=True, stop=True)
            pe.wait_ge(s_sw, 32)
            for c in range(C):
                for k in range(C):
                    mm = nc.tensor.matmul(ps_m[:, 0, 2 * c:2 * c + 2], wvt_sb[:, k, c * P:(c + 1) * P],
                                          awbv_sb[:, k, 0:2], start=(k == 0), stop=(k == C - 1))
            mm.then_inc(s_ws, 1)
            pe.wait_ge(s_ab, 16)
            pe.wait_ge(s_cp, 1)
            nc.tensor.matmul(ps_z[:, 1, 0:3], ones[:, :], cprod[:, 0:3], start=True, stop=True).then_inc(s_cs, 1)
            pe.wait_ge(s_w2s, 1)
            pe.wait_ge(s_id, 1)

            def halves(acc, st_hi, st_lo, mv_hi, mv_lo, start, stop):
                nc.tensor.matmul(acc(mv_hi), st_hi, mv_hi, start=start, stop=False, skip_group_check=True)
                nc.tensor.matmul(acc(mv_lo), st_hi, mv_lo, start=False, stop=False, skip_group_check=True)
                return nc.tensor.matmul(acc(mv_hi), st_lo, mv_hi, start=False, stop=stop, skip_group_check=True)

            def project2(r, k):
                pe.wait_ge(s_xt_hi, r + 1)
                for g in range(GP):
                    pe.wait_ge(s_xt_lo[g], r + 1)
                    wait_count(pe, s_xw2_lo[g], r)
                    for c in range(C):
                        cols = slice((g * C + c) * P, (g * C + c + 1) * P)
                        mm = halves(lambda m: ps_m[:, g, 0:m.shape[-1]], xt_hi[:, k, cols], xt_lo[:, k, cols],
                                    w2s_hi[:, c, :], w2s_lo[:, c, :], c == 0, c == C - 1)
                    mm.then_inc(s_xw2[g], 1)

            def project01(r, k, g):
                wait_count(pe, s_hb, r)
                for c in range(C):
                    cols = slice((g * C + c) * P, (g * C + c + 1) * P)
                    mm = halves(lambda m: ps_z[:, g, 0:m.shape[-1]], xt_hi[:, k, cols], xt_lo[:, k, cols],
                                w01_hi[:, c, :], w01_lo[:, c, :], c == 0, False)
                if g == GP - 1:
                    mm.then_inc(s_xt_used, 1)

            def spread_source(r):
                pe.wait_ge(s_score, r + 1)
                wait_count(pe, s_tt_lo, r)
                for g in range(GP):
                    mm = nc.tensor.transpose(ps_u[:, 0, g, :], score[:, g, 0:1].to_broadcast([P, P]), ident[:, :])
                mm.then_inc(s_u, 1)

            def transpose_t(r):
                pe.wait_ge(s_trans, r + 1)
                for g in range(GP):
                    mm = nc.tensor.transpose(ps_u[:, 1, g, :], trans[:, g, :], ident[:, :])
                mm.then_inc(s_tt, 1)

            def hop1(r, k):
                pe.wait_ge(s_tt_hi, r + 1)
                pe.wait_ge(s_tt_lo, r + 1)
                for g in range(GP):
                    pe.wait_ge(s_xw2_hi[g], r + 1)
                    pe.wait_ge(s_xw2_lo[g], r + 1)
                    halves(lambda m: ps_z[:, g, D:2 * D], tt_hi[:, g, :], tt_lo[:, g, :],
                           xw2_hi[:, k, g, :], xw2_lo[:, k, g, :], False, False).then_inc(s_z[g], 1)

            def hop2(r):
                for g in range(GP):
                    pe.wait_ge(s_z_hi[g], r + 1)
                    pe.wait_ge(s_z_lo[g], r + 1)
                    halves(lambda m: ps_z[:, g, 0:D], tt_hi[:, g, :], tt_lo[:, g, :],
                           z_hi[:, g, :], z_lo[:, g, :], False, True).then_inc(s_h[g], 1)

            def transpose_x1(r, k):
                wait_count(pe, s_x1t_lo, r)
                for g in range(GP):
                    pe.wait_ge(s_x1[g], r + 1)
                    for c in range(C):
                        mm = nc.tensor.transpose(ps_x[:, g, c, :], x1[:, k, g, c * P:(c + 1) * P], ident[:, :])
                mm.then_inc(s_x1t, 1)

            def project_x1_high(r, g, chunks):
                pe.wait_ge(s_x1t_hi[g], r + 1)
                if at(r, NP - 2):
                    pe.wait_ge(s_xw2_lo[g], NP)
                    pe.wait_ge(s_score, NP)
                elif at(r, NP - 1):
                    pe.wait_ge(s_o[g], r - 1)
                else:
                    wait_count(pe, s_o[g], r)
                for c in chunks:
                    for w in (w1_hi, w1_lo):
                        nc.tensor.matmul(bank2(r)[:, g, :], x1t_hi[:, g, c, :], w[:, c, :],
                                         start=(c == 0 and w is w1_hi), stop=False, skip_group_check=True)

            def project_x1_low(r, g):
                pe.wait_ge(s_x1t_lo, r + 1)
                for c in range(C):
                    mm = nc.tensor.matmul(bank2(r)[:, g, :], x1t_lo[:, g, c, :], w1_hi[:, c, :], start=False,
                                          stop=(c == C - 1), skip_group_check=True)
                mm.then_inc(s_pq[g], 1)

            def project_x1_hop2(r, hop):
                project_x1_high(r, 0, range(C))
                project_x1_high(r, 1, range(1))
                project_x1_low(r, 0)
                hop2(hop)
                project_x1_high(r, 1, range(1, C))
                project_x1_low(r, 1)

            def aggregate(r, k):
                pe.wait_ge(s_adjt_hi, r + 1)
                pe.wait_ge(s_adjt_lo, r + 1)
                for g in range(GP):
                    pe.wait_ge(s_self[g], r + 1)
                    pe.wait_ge(s_q_hi[g], r + 1)
                    pe.wait_ge(s_q_lo[g], r + 1)
                    cols = slice(g * P, (g + 1) * P)
                    halves(lambda m: bank2(r)[:, g, 0:m.shape[-1]], adjt_hi[:, k, cols], adjt_lo[:, k, cols],
                           q_hi[:, g, :], q_lo[:, g, :], True, True).then_inc(s_agg[g], 1)

            def step(p, k):
                if there(p + 1):
                    project2(p + 1, 1 - k)
                first = at(p, 0)
                if at(p, -1):
                    pe.wait_ge(s_bk, 16)
                    nc.tensor.matmul(ps_q[:, 0, 0:D], ones[:, :], bk_raw[:, :], start=True,
                                     stop=True).then_inc(s_bsum, 1)
                    spread_source(0)
                    pe.wait_ge(s_w01, 1)
                    project01(0, 0, 0)
                if first:
                    project01(0, 0, 1)
                elif there(p):
                    project01(p, k, 0)
                if there(p - 2):
                    aggregate(p - 2, k)
                if there(p):
                    transpose_t(p)
                    if not first:
                        project01(p, k, 1)
                if there(p - 1):
                    transpose_x1(p - 1, 1 - k)
                if there(p):
                    hop1(p, k)
                if there(p + 1) and not (at(p, -1)):
                    spread_source(p + 1)
                if at(p, 1):
                    pe.wait_ge(s_w1, 1)
                    pe.wait_ge(s_bias, 1)
                if there(p - 1) and there(p):
                    project_x1_hop2(p - 1, p)
                elif there(p):
                    hop2(p)

            def last(p, k):
                if p == NP - 1:
                    project01(p, k, 0)
                    transpose_t(p)
                    project01(p, k, 1)
                    hop1(p, k)
                    aggregate(p - 2, k)
                    hop2(p)
                    transpose_x1(p - 1, 1 - k)
                else:
                    for _ in range(KEEP_UP):
                        nc.tensor.matmul(ps_z[:, 0, :], x1t_hi[:, 0, 0, :], w1_hi[:, 0, :], start=True, stop=True)
                    transpose_x1(p - 1, 1 - k)
                    aggregate(p - 2, k)
                for g in range(GP):
                    project_x1_high(p - 1, g, range(C))
                    project_x1_low(p - 1, g)

            steps(pe, step, last)

        @block.scalar
        def _(act):
            def copy_score(r):
                act.wait_ge(s_xw2[0], r + 1)
                act.wait_ge(s_xw2[1], r + 1)
                wait_count(act, s_u, r)
                nc.scalar.activation(score[:, :, :], ps_m[:, :, D:D + 2], ACT.Identity,
                                     bias=chalf[:, 0:1]).then_inc(s_score, 1)

            def split_xw2(r, k, g):
                wait_count(act, s_z[g], r - 1)
                nc.scalar.activation(xw2_hi[:, k, g, :], ps_m[:, g, 0:D], ACT.Copy).then_inc(s_xw2_hi[g], 1)

            def split_tt(r):
                act.wait_ge(s_tt, r + 1)
                wait_count(act, s_h[1], r)
                nc.scalar.activation(tt_hi[:, :, :], ps_u[:, 1, :, :], ACT.Copy).then_inc(s_tt_hi, 1)

            def split_adjt(r, k):
                act.wait_ge(adjt_in[k], dma_count(r, k))
                wait_count(act, s_agg[1], r - 1)
                nc.scalar.activation(adjt_hi[:, k, :], adjt_raw[:, k, :], ACT.Copy).then_inc(s_adjt_hi, 1)

            def split_x1t(r):
                act.wait_ge(s_x1t, r + 1)
                wait_count(act, s_pq[1], r)
                for g in range(GP):
                    nc.scalar.activation(x1t_hi[:, g, :, :], ps_x[:, g, :, :], ACT.Copy).then_inc(s_x1t_hi[g], 1)

            def add_scores(r):
                act.wait_ge(s_u, r + 1)
                act.wait_ge(s_score, r + 1)
                wait_count(act, s_leaky, r)
                for g in range(GP):
                    a = nc.scalar.activation(e_sum[:, g, :], ps_u[:, 0, g, :], ACT.Identity,
                                             bias=score[:, g, 1:2])
                a.then_inc(s_esum, 1)

            def split_z(r, g):
                act.wait_ge(s_z[g], r + 1)
                wait_count(act, s_h[g], r)
                nc.scalar.activation(z_hi[:, g, :], ps_z[:, g, D:2 * D], ACT.Copy).then_inc(s_z_hi[g], 1)

            def square_y2(r, k):
                act.wait_ge(s_nmean2, r + 1)
                wait_count(act, s_var2, r - 1)
                for g in range(GP):
                    wait_count(act, s_sq2[g], r)
                    nc.scalar.activation(sq_out[:, g, :], y2[:, k, g, :], ACT.Square, bias=nmean2[:, k, g:g + 1],
                                         accum_out=sq2[:, k, g:g + 1]).then_inc(s_sq2[g], 1)

            def split_xt(r, k):
                act.wait_ge(xt_in[k], dma_count(r, k))
                wait_count(act, s_xt_used, r - 1)
                nc.scalar.activation(xt_hi[:, k, :], xt_raw[:, k, :], ACT.Copy).then_inc(s_xt_hi, 1)

            def exponential(r):
                act.wait_ge(s_leaky, r + 1)
                wait_count(act, s_alpha, r)
                nc.scalar.activation(e_exp[:, :, :], e_leaky[:, :].rearrange("p (g n) -> p g n", g=GP),
                                     ACT.Exp).then_inc(s_exp, 1)

            def split_q(r, g):
                act.wait_ge(s_pq[g], r + 1)
                wait_count(act, s_o[g], r)
                nc.scalar.activation(self_sb[:, g, :], bank2(r)[:, g, 0:D], ACT.Copy).then_inc(s_self[g], 1)
                wait_count(act, s_agg[g], r)
                nc.scalar.activation(q_hi[:, g, 0:D], bank2(r)[:, g, D:2 * D], ACT.Copy).then_inc(s_q_hi[g], 1)

            def scale_rows(r):
                act.wait_ge(s_rowinv, r + 1)
                wait_count(act, s_tt, r)
                for g in range(GP):
                    a = nc.scalar.activation(trans[:, g, :], alpha[:, g, :], ACT.Copy, scale=rowinv[:, g:g + 1])
                a.then_inc(s_trans, 1)

            act.dma_start(wvt_sb[:], wvt).then_inc(s_sw, 16)
            act.dma_start(awbv_sb[:], awbv).then_inc(s_sw, 16)
            act.dma_start(wk_raw[:, :, 0:2 * D], wk[:, :, 0:2 * D]).then_inc(s_w01_in, 16)
            act.wait_ge(s_const, 1)
            nc.scalar.activation(table_out[:, :], ones[:, 0:1], ACT.Exp)

            def step(p, k):
                filling = isinstance(p, int) and p < 0
                if filling and there(p + 2):
                    split_xt(p + 2, k)
                if at(p, -1):
                    act.wait_ge(s_w01_in, 16)
                    nc.scalar.activation(w01_hi[:, :, :], wk_raw[:, :, 0:2 * D], ACT.Copy).then_inc(s_w01_hi, 1)
                    act.wait_ge(s_chalf, 1)
                if there(p + 1):
                    copy_score(p + 1)
                    split_xw2(p + 1, 1 - k, 0)
                    split_xw2(p + 1, 1 - k, 1)
                if there(p):
                    split_tt(p)
                if at(p, 0):
                    split_xt(2, 0)
                    act.wait_ge(s_w1_in, 16)
                    nc.scalar.activation(w1_hi[:, :, :], w1_raw[:, :, :], ACT.Copy).then_inc(s_w1_hi, 1)
                if there(p - 1):
                    split_adjt(p - 1, 1 - k)
                if there(p - 3):
                    square_y2(p - 3, 1 - k)
                if there(p - 1):
                    split_x1t(p - 1)
                if there(p):
                    split_z(p, 0)
                    split_z(p, 1)
                if there(p + 1):
                    add_scores(p + 1)
                if not (isinstance(p, int) and p <= 0) and there(p + 2):
                    split_xt(p + 2, k)
                if there(p + 1):
                    exponential(p + 1)
                if there(p - 1):
                    split_q(p - 1, 0)
                    split_q(p - 1, 1)
                if there(p + 1):
                    scale_rows(p + 1)

            def last(p, k):
                if p == NP - 1:
                    split_tt(p)
                    square_y2(p - 3, 1 - k)
                    split_z(p, 0)
                    split_z(p, 1)
                    split_adjt(p - 1, 1 - k)
                    split_x1t(p - 1)
                else:
                    split_x1t(p - 1)
                    split_adjt(p - 1, 1 - k)
                    square_y2(p - 3, 1 - k)
                split_q(p - 1, 0)
                split_q(p - 1, 1)

            steps(act, step, last)
            k = (NP - 1) % 2
            act.wait_ge(stored[k], dma_count(NP - 3, k))
            act.wait_ge(s_shift2, NP)
            nc.scalar.activation(out_sb[:, k, 1, :], y2[:, k, 1, :], ACT.Identity, bias=shift2[:, k, 1:2],
                                 scale=rstd2[:, k, 1:2]).then_inc(s_out_last, 1)

        @block.gpsimd
        def _(pool):
            nc.gpsimd.memset(cprod[:], 0.0).then_inc(s_zero, 1)
            nc.gpsimd.memset(bk_raw[:], 0.0).then_inc(s_zero, 1)
            pool.wait_ge(s_zero, 2)
            pool.dma_start(cprod[0:1, 2:3], ab).then_inc(s_ab, 16)
            pool.dma_start(bk_raw[0:3, :], bk).then_inc(s_bk, 16)
            nc.gpsimd.memset(ident[:], 0.0).then_inc(s_fill, 1)
            nc.gpsimd.memset(half[:], -0.5).then_inc(s_fill, 1)
            pool.wait_ge(s_fill, 2)
            nc.gpsimd.affine_select(out=ident[:], in_=ident[:], compare_op=ALU.not_equal, fill=1.0, base=0,
                                    pattern=[[-1, P]], channel_multiplier=1).then_inc(s_id, 1)

            def rstd_of_y1(r):
                pool.wait_ge(s_var1, r + 1)
                wait_count(pool, s_x1[1], r)
                nc.gpsimd.tensor_tensor(rstd1[:, :], var1[:, :], half[:, :], ALU.pow).then_inc(s_rstd1, 1)

            def split_adjt(r, k):
                pool.wait_ge(s_adjt_hi, r + 1)
                wait_count(pool, s_agg[1], r - 1)
                nc.gpsimd.tensor_tensor(adjt_lo[:, k, :], adjt_raw[:, k, :], adjt_hi[:, k, :].bitcast(F32),
                                        ALU.subtract).then_inc(s_adjt_lo, 1)

            def y2_scale_ready(r, k):
                wait_count(pool, stored[k], dma_count(r - 2, k))
                pool.wait_ge(s_shift2, r + 1)

            def normalise_y2(r, k):
                for g in range(GP):
                    t = nc.gpsimd.tensor_scalar(out_sb[:, k, g, :], y2[:, k, g, :], rstd2[:, k, g:g + 1],
                                                shift2[:, k, g:g + 1], ALU.mult, ALU.add)
                t.then_inc(s_out, 1)

            def split_xt(r, k):
                pool.wait_ge(s_xt_hi, r + 1)
                wait_count(pool, s_xt_used, r - 1)
                for g in range(GP):
                    cols = slice(g * C * P, (g + 1) * C * P)
                    nc.gpsimd.tensor_tensor(xt_lo[:, k, cols], xt_raw[:, k, cols], xt_hi[:, k, cols].bitcast(F32),
                                            ALU.subtract).then_inc(s_xt_lo[g], 1)

            def rstd_of_y2(r, k):
                pool.wait_ge(s_var2, r + 1)
                nc.gpsimd.tensor_tensor(rstd2[:, k, :], var2[:, k, :], half[:, :], ALU.pow).then_inc(s_rstd2, 1)
                pool.wait_ge(s_rstd2, r + 1)
                nc.gpsimd.tensor_tensor(shift2[:, k, :], rstd2[:, k, :], nmean2[:, k, :],
                                        ALU.mult).then_inc(s_shift2, 1)

            def step(p, k):
                if there(p - 1):
                    rstd_of_y1(p - 1)
                    split_adjt(p - 1, 1 - k)
                if there(p - 3):
                    rstd_of_y2(p - 3, 1 - k)
                if there(p - 3) and not at(p - 3, NP - 1):
                    y2_scale_ready(p - 3, 1 - k)
                if there(p + 2):
                    split_xt(p + 2, k)
                if at(p, 0):
                    pool.wait_ge(s_w1_hi, 1)
                    nc.gpsimd.tensor_tensor(w1_lo[:, :, :], w1_raw[:, :, :], w1_hi[:, :, :].bitcast(F32),
                                            ALU.subtract).then_inc(s_w1, 1)
                if there(p - 3) and not at(p - 3, NP - 1):
                    normalise_y2(p - 3, 1 - k)

            steps(pool, step, step)

        @block.vector
        def _(dve):
            links = [0]

            def link(ins):
                links[0] += 1
                ins.then_inc(s_dset, 1)
                dve.wait_ge(s_dset, links[0])

            nc.vector.memset(ones[:], 1.0).then_inc(s_const, 1)
            dve.wait_ge(s_const, 1)
            for g in range(GP):
                link(nc.vector.tensor_copy(q_hi[:, g, D:D + 2], ones[:, 0:2]))
            dve.wait_ge(s_sw, 32)
            dve.wait_ge(s_zero, 2)
            link(nc.vector.tensor_tensor(cprod[:, 0:C], awbv_sb[:, :, 0], awbv_sb[:, :, 1], ALU.add))
            nc.vector.tensor_tensor(cprod[:, 0:C], cprod[:, 0:C], awbv_sb[:, :, 2], ALU.mult).then_inc(s_cp, 1)
            dve.wait_ge(s_w2_in, 16)
            w2 = wk_raw[:, :, 2 * D:3 * D]
            link(nc.vector.tensor_copy(w2s_hi[:, :, 0:D], w2))
            nc.vector.tensor_tensor(w2s_lo[:, :, 0:D], w2, w2s_hi[:, :, 0:D].bitcast(F32), ALU.subtract)
            dve.wait_ge(s_ws, 1)
            ws = ps_m[:, 0, 0:2 * C].rearrange("p (c s) -> p c s", c=C)
            link(nc.vector.tensor_copy(w2s_hi[:, :, D:D + 2], ws))
            nc.vector.tensor_tensor(w2s_lo[:, :, D:D + 2], ws,
                                    w2s_hi[:, :, D:D + 2].bitcast(F32), ALU.subtract).then_inc(s_w2s, 1)
            dve.wait_ge(s_cs, 1)
            link(nc.vector.reduce_sum(chalf[:, :], ps_z[:, 1, 0:3], axis=mybir.AxisListType.X))
            nc.vector.tensor_scalar(chalf[:, :], chalf[:, :], 0.5, None, ALU.mult).then_inc(s_chalf, 1)
            dve.wait_ge(s_w01_hi, 1)
            nc.vector.tensor_tensor(w01_lo[:, :, :], wk_raw[:, :, 0:2 * D], w01_hi[:, :, :].bitcast(F32),
                                    ALU.subtract).then_inc(s_w01, 1)

            def add_bias(r):
                dve.wait_ge(s_h[0], r + 1)
                dve.wait_ge(s_h[1], r + 1)
                nc.vector.tensor_tensor(hb[:, :, :], ps_z[:, :, 0:D],
                                        bias[:, :].unsqueeze(1).to_broadcast([P, GP, D]), ALU.add).then_inc(s_hb, 1)

            def residual1(r, k, g):
                dve.wait_ge(x_in[k], dma_count(r, k))
                dve.wait_ge(s_hb, r + 1)
                wait_count(dve, s_x1[1], r)
                nc.vector.scalar_tensor_tensor(out=y1[:, g, :], in0=hb[:, g, :], scalar=0.0,
                                               in1=x_sb[:, k, g * D:(g + 1) * D], op0=ALU.max,
                                               op1=ALU.add).then_inc(s_y1[g], 1)

            def statistics1(r):
                for g in range(GP):
                    dve.wait_ge(s_y1[g], r + 1)
                    nc.vector.bn_stats(bn6[:, g, :], y1[:, g, :]).then_inc(s_bn[g], 1)

            def stats1_written(r):
                dve.wait_ge(s_bn[0], r + 1)
                dve.wait_ge(s_bn[1], r + 1)

            def moments1(r):
                for g in range(GP):
                    nc.vector.bn_aggr(mv[:, g, :], bn6[:, g, :]).then_inc(s_mv[g], 1)
                dve.wait_ge(s_mv[0], r + 1)
                dve.wait_ge(s_mv[1], r + 1)
                wait_count(dve, s_rstd1, r)
                nc.vector.tensor_scalar(var1[:, :], mv[:, :, 1], LN_EPS, None, ALU.add).then_inc(s_var1, 1)

            def split_xw2(r, k, g):
                dve.wait_ge(s_score, r + 1)
                dve.wait_ge(s_xw2_hi[g], r + 1)
                wait_count(dve, s_z[g], r - 1)
                nc.vector.tensor_tensor(xw2_lo[:, k, g, :], ps_m[:, g, 0:D], xw2_hi[:, k, g, :].bitcast(F32),
                                        ALU.subtract).then_inc(s_xw2_lo[g], 1)

            def split_tt(r):
                dve.wait_ge(s_tt_hi, r + 1)
                wait_count(dve, s_h[1], r)
                nc.vector.tensor_tensor(tt_lo[:, :, :], ps_u[:, 1, :, :], tt_hi[:, :, :].bitcast(F32),
                                        ALU.subtract).then_inc(s_tt_lo, 1)

            def normalise_y1(r, k):
                dve.wait_ge(s_rstd1, r + 1)
                wait_count(dve, s_x1t, r - 1)
                for g in range(GP):
                    nc.vector.tensor_scalar(x1[:, k, g, :], y1[:, g, :], mv[:, g, 0:1], rstd1[:, g:g + 1],
                                            ALU.subtract, ALU.mult).then_inc(s_x1[g], 1)

            def degree(r):
                dve.wait_ge(s_agg[0], r + 1)
                dve.wait_ge(s_agg[1], r + 1)
                nc.vector.tensor_scalar(deg[:, :], bank2(r)[:, :, D], DEG_EPS, None, ALU.max).then_inc(s_deg, 1)

            def degree_inverse(r):
                dve.wait_ge(s_deg, r + 1)
                nc.vector.reciprocal(deginv[:, :], deg[:, :]).then_inc(s_deginv, 1)

            def add_aggregate(r):
                dve.wait_ge(s_deginv, r + 1)
                for g in range(GP):
                    dve.wait_ge(s_self[g], r + 1)
                    nc.vector.scalar_tensor_tensor(out=o_sum[:, g, :], in0=bank2(r)[:, g, 0:D],
                                                   scalar=deginv[:, g:g + 1], in1=self_sb[:, g, :],
                                                   op0=ALU.mult, op1=ALU.add).then_inc(s_o[g], 1)

            def residual2(r, k):
                wait_count(dve, s_out, r - 1)
                wait_count(dve, s_sq2[1], r - 1)
                for g in range(GP):
                    dve.wait_ge(s_o[g], r + 1)
                    nc.vector.scalar_tensor_tensor(out=y2[:, k, g, :], in0=o_sum[:, g, :], scalar=0.0,
                                                   in1=x1[:, k, g, :], op0=ALU.max, op1=ALU.add,
                                                   accum_out=sum2[:, k, g:g + 1]).then_inc(s_y2[g], 1)

            def mean2(r, k):
                dve.wait_ge(s_y2[0], r + 1)
                dve.wait_ge(s_y2[1], r + 1)
                wait_count(dve, s_shift2, r - 1)
                nc.vector.tensor_scalar(nmean2[:, k, :], sum2[:, k, :], -1.0 / D, None,
                                        ALU.mult).then_inc(s_nmean2, 1)

            def split_x1t(r):
                dve.wait_ge(s_x1t_hi[0], r + 1)
                dve.wait_ge(s_x1t_hi[1], r + 1)
                wait_count(dve, s_pq[1], r)
                nc.vector.tensor_tensor(x1t_lo[:, :, :, :], ps_x[:, :, :, :], x1t_hi[:, :, :, :].bitcast(F32),
                                        ALU.subtract).then_inc(s_x1t_lo, 1)

            def leaky(r):
                dve.wait_ge(s_esum, r + 1)
                wait_count(dve, s_exp, r)
                e = e_sum[:, :, :].rearrange("p g n -> p (g n)")
                nc.vector.scalar_tensor_tensor(out=e_leaky[:, :], in0=e, scalar=LEAK, in1=e, op0=ALU.mult,
                                               op1=ALU.max).then_inc(s_leaky, 1)

            def split_z(r, g):
                dve.wait_ge(s_z_hi[g], r + 1)
                wait_count(dve, s_h[g], r)
                nc.vector.tensor_tensor(z_lo[:, g, :], ps_z[:, g, D:2 * D], z_hi[:, g, :].bitcast(F32),
                                        ALU.subtract).then_inc(s_z_lo[g], 1)

            def weigh(r, k):
                dve.wait_ge(adj_in[k], dma_count(r, k))
                dve.wait_ge(s_exp, r + 1)
                wait_count(dve, s_trans, r)
                for g in range(GP):
                    a = nc.vector.tensor_tensor_reduce(alpha[:, g, :], adj_sb[:, k, g * P:(g + 1) * P],
                                                       e_exp[:, g, :], 1.0, ROW_EPS, ALU.mult, ALU.add,
                                                       rowsum[:, g:g + 1])
                a.then_inc(s_alpha, 1)

            def invert_rows(r):
                dve.wait_ge(s_alpha, r + 1)
                nc.vector.reciprocal(rowinv[:, :], rowsum[:, :]).then_inc(s_rowinv, 1)

            def variance2(r, k):
                dve.wait_ge(s_sq2[0], r + 1)
                dve.wait_ge(s_sq2[1], r + 1)
                wait_count(dve, s_rstd2, r - 1)
                nc.vector.tensor_scalar(var2[:, k, :], sq2[:, k, :], 1.0 / D, LN_EPS, ALU.mult,
                                        ALU.add).then_inc(s_var2, 1)

            def split_q(r, g):
                dve.wait_ge(s_q_hi[g], r + 1)
                wait_count(dve, s_agg[g], r)
                nc.vector.tensor_tensor(q_lo[:, g, :], bank2(r)[:, g, D:2 * D], q_hi[:, g, 0:D].bitcast(F32),
                                        ALU.subtract).then_inc(s_q_lo[g], 1)

            def step(p, k):
                if there(p - 1):
                    statistics1(p - 1)
                if there(p - 2):
                    split_q(p - 2, 1)
                if there(p - 1):
                    stats1_written(p - 1)
                if there(p - 3):
                    mean2(p - 3, 1 - k)
                if there(p - 1):
                    moments1(p - 1)
                if there(p + 1):
                    split_xw2(p + 1, 1 - k, 0)
                    split_xw2(p + 1, 1 - k, 1)
                if there(p - 1):
                    normalise_y1(p - 1, 1 - k)
                if there(p):
                    split_tt(p)
                if there(p - 2):
                    degree(p - 2)
                if there(p - 2):
                    degree_inverse(p - 2)
                if there(p - 2):
                    add_aggregate(p - 2)
                if there(p - 1):
                    split_x1t(p - 1)
                if there(p - 3):
                    variance2(p - 3, 1 - k)
                if there(p):
                    split_z(p, 0)
                    split_z(p, 1)
                if there(p + 1):
                    leaky(p + 1)
                if there(p - 2):
                    residual2(p - 2, k)
                if at(p, -1):
                    dve.wait_ge(s_bsum, 1)
                    nc.vector.tensor_copy(bias[:, :], ps_q[:, 0, 0:D]).then_inc(s_bias, 1)
                if there(p):
                    if at(p, 0):
                        dve.wait_ge(s_bias, 1)
                    add_bias(p)
                if there(p + 1):
                    weigh(p + 1, 1 - k)
                if there(p):
                    residual1(p, k, 0)
                if there(p + 1):
                    invert_rows(p + 1)
                if there(p):
                    residual1(p, k, 1)
                if there(p - 1) and not at(p, NP - 2):
                    split_q(p - 1, 0)

            def last(p, k):
                if p == NP - 1:
                    statistics1(p - 1)
                    mean2(p - 3, 1 - k)
                    stats1_written(p - 1)
                    split_tt(p)
                    moments1(p - 1)
                    split_q(p - 2, 0)
                    split_q(p - 2, 1)
                    split_z(p, 0)
                    split_z(p, 1)
                    normalise_y1(p - 1, 1 - k)
                    degree(p - 2)
                    variance2(p - 3, 1 - k)
                    degree_inverse(p - 2)
                    add_bias(p)
                    add_aggregate(p - 2)
                    split_x1t(p - 1)
                    residual1(p, k, 0)
                    residual1(p, k, 1)
                    statistics1(p)
                    stats1_written(p)
                    moments1(p)
                    residual2(p - 2, k)
                    split_q(p - 1, 0)
                    mean2(p - 2, k)
                else:
                    normalise_y1(p - 1, 1 - k)
                    split_q(p - 2, 1)
                    split_x1t(p - 1)
                    degree(p - 2)
                    degree_inverse(p - 2)
                    add_aggregate(p - 2)
                    variance2(p - 3, 1 - k)
                    split_q(p - 1, 0)
                    residual2(p - 2, k)

            steps(dve, step, last)
            k = (NP - 1) % 2
            dve.wait_ge(stored[k], dma_count(NP - 3, k))
            dve.wait_ge(s_shift2, NP)
            nc.vector.tensor_scalar(out_sb[:, k, 0, :], y2[:, k, 0, :], rstd2[:, k, 0:1], shift2[:, k, 0:1],
                                    ALU.mult, ALU.add).then_inc(s_out_last, 1)


def kernel(x, adj, L0_gnn_Wv, L0_gnn_bv, L0_gnn_aw, L0_gnn_ab, L0_gnn_Wk, L0_gnn_bk, L1_gnn_W):
    import numpy as np
    import concourse.bacc as bacc
    from concourse.bass_utils import run_bass_kernel_spmd

    x, adj = np.asarray(x), np.asarray(adj)
    Wv, bv, aw, ab = (np.asarray(a) for a in (L0_gnn_Wv, L0_gnn_bv, L0_gnn_aw, L0_gnn_ab))
    Wk, bk, W1 = np.asarray(L0_gnn_Wk), np.asarray(L0_gnn_bk), np.asarray(L1_gnn_W)
    B = x.shape[0]
    NP = B // GP

    def rows(a):
        return a.reshape(C, P, -1).transpose(1, 0, 2)

    arrays = {
        "in_xt": x.reshape(NP, GP, P, C, P).transpose(0, 4, 1, 3, 2).reshape(NP, P, GP * C * P),
        "in_adj": adj.reshape(NP, GP, P, P).transpose(0, 2, 1, 3).reshape(NP, P, GP * P),
        "in_x": x.reshape(NP, GP, P, D).transpose(0, 2, 1, 3).reshape(NP, P, GP * D),
        "in_adjt": adj.reshape(NP, GP, P, P).transpose(0, 3, 1, 2).reshape(NP, P, GP * P),
        "in_wk": rows(Wk.transpose(1, 0, 2).reshape(D, 3 * D)),
        "in_wvt": rows(Wv.T),
        "in_awbv": rows(np.concatenate([aw.reshape(2, D), bv.reshape(1, D)]).T),
        "in_ab": ab.reshape(1, 1),
        "in_bk": bk,
        "in_w1": rows(W1.reshape(D, 2, D).transpose(2, 1, 0).reshape(D, 2 * D)),
    }
    arrays = {n: np.ascontiguousarray(a) for n, a in arrays.items()}
    nc = bacc.Bacc("TRN2", target_bir_lowering=False, num_devices=1)
    args = [nc.dram_tensor(n, a.shape, mybir.dt.from_np(a.dtype), kind="ExternalInput").ap()
            for n, a in arrays.items()]
    args.append(nc.dram_tensor("out_y", (NP, P, GP * D), F32, kind="ExternalOutput").ap())
    graph_layers_kernel(nc, *args)
    got = run_bass_kernel_spmd(nc, [arrays], core_ids=[0]).results[0]["out_y"]
    return got.reshape(NP, P, GP, D).transpose(0, 2, 1, 3).reshape(B, P, D)
```
